# Optimizing a Trainium2 kernel written in Bass

```python
import numpy as np
import jax
import jax.numpy as jnp

def _softmax(x, axis=-1):
    return jax.nn.softmax(x, axis=axis)

def _gelu(x):
    return jax.nn.gelu(x, approximate=True)

def _silu(x):
    return jax.nn.silu(x)

def _sigmoid(x):
    return jax.nn.sigmoid(x)

def _layernorm(x, axis=-1, eps=1e-05):
    m = jnp.mean(x, axis=axis, keepdims=True)
    v = jnp.var(x, axis=axis, keepdims=True)
    return (x - m) / jnp.sqrt(v + eps)

def _scatter_add(tgt, idx, src, axis=0):
    return tgt.at[idx].add(src)

def _segment_sum(src, seg, n):
    return jax.ops.segment_sum(src, seg, n)
kernel_name = 'mk_dlrm_tower_d1_rec_r8_613f3c'

def setup_inputs(seed: int=0):
    np.random.seed(seed)
    _w = jnp.asarray

    def _rec_inputs():
        import jax
        import jax.numpy as jnp
        _tk = jax.random.key(seed)
        dense_ctx = jax.random.normal(jax.random.fold_in(_tk, 190), (2048, 16), jnp.float32)
        ids = jnp.stack([jax.random.randint(jax.random.fold_in(_tk, 200 + f), (2048,), 0, v, jnp.int32) for f, v in enumerate([12500, 125000, 1250, 1250, 1000, 1250, 1250, 1000, 12500, 1250, 1250, 1000, 12500, 1000, 1250, 12500, 12500, 125000, 1000, 12500, 1000, 1250, 1000, 125000, 12500, 12500, 1000, 1000, 1250, 1000, 125000, 1000])], axis=1)
        tbl_0 = 0.05 * jax.random.normal(jax.random.fold_in(_tk, 500 + 0), (12500, 16), jnp.float32)
        tbl_1 = 0.05 * jax.random.normal(jax.random.fold_in(_tk, 500 + 1), (125000, 16), jnp.float32)
        tbl_2 = 0.05 * jax.random.normal(jax.random.fold_in(_tk, 500 + 2), (1250, 16), jnp.float32)
        tbl_3 = 0.05 * jax.random.normal(jax.random.fold_in(_tk, 500 + 3), (1250, 16), jnp.float32)
        tbl_4 = 0.05 * jax.random.normal(jax.random.fold_in(_tk, 500 + 4), (1000, 16), jnp.float32)
        tbl_5 = 0.05 * jax.random.normal(jax.random.fold_in(_tk, 500 + 5), (1250, 16), jnp.float32)
        tbl_6 = 0.05 * jax.random.normal(jax.random.fold_in(_tk, 500 + 6), (1250, 16), jnp.float32)
        tbl_7 = 0.05 * jax.random.normal(jax.random.fold_in(_tk, 500 + 7), (1000, 16), jnp.float32)
        tbl_8 = 0.05 * jax.random.normal(jax.random.fold_in(_tk, 500 + 8), (12500, 16), jnp.float32)
        tbl_9 = 0.05 * jax.random.normal(jax.random.fold_in(_tk, 500 + 9), (1250, 16), jnp.float32)
        tbl_10 = 0.05 * jax.random.normal(jax.random.fold_in(_tk, 500 + 10), (1250, 16), jnp.float32)
        tbl_11 = 0.05 * jax.random.normal(jax.random.fold_in(_tk, 500 + 11), (1000, 16), jnp.float32)
        tbl_12 = 0.05 * jax.random.normal(jax.random.fold_in(_tk, 500 + 12), (12500, 16), jnp.float32)
        tbl_13 = 0.05 * jax.random.normal(jax.random.fold_in(_tk, 500 + 13), (1000, 16), jnp.float32)
        tbl_14 = 0.05 * jax.random.normal(jax.random.fold_in(_tk, 500 + 14), (1250, 16), jnp.float32)
        tbl_15 = 0.05 * jax.random.normal(jax.random.fold_in(_tk, 500 + 15), (12500, 16), jnp.float32)
        tbl_16 = 0.05 * jax.random.normal(jax.random.fold_in(_tk, 500 + 16), (12500, 16), jnp.float32)
        tbl_17 = 0.05 * jax.random.normal(jax.random.fold_in(_tk, 500 + 17), (125000, 16), jnp.float32)
        tbl_18 = 0.05 * jax.random.normal(jax.random.fold_in(_tk, 500 + 18), (1000, 16), jnp.float32)
        tbl_19 = 0.05 * jax.random.normal(jax.random.fold_in(_tk, 500 + 19), (12500, 16), jnp.float32)
        tbl_20 = 0.05 * jax.random.normal(jax.random.fold_in(_tk, 500 + 20), (1000, 16), jnp.float32)
        tbl_21 = 0.05 * jax.random.normal(jax.random.fold_in(_tk, 500 + 21), (1250, 16), jnp.float32)
        tbl_22 = 0.05 * jax.random.normal(jax.random.fold_in(_tk, 500 + 22), (1000, 16), jnp.float32)
        tbl_23 = 0.05 * jax.random.normal(jax.random.fold_in(_tk, 500 + 23), (125000, 16), jnp.float32)
        tbl_24 = 0.05 * jax.random.normal(jax.random.fold_in(_tk, 500 + 24), (12500, 16), jnp.float32)
        tbl_25 = 0.05 * jax.random.normal(jax.random.fold_in(_tk, 500 + 25), (12500, 16), jnp.float32)
        tbl_26 = 0.05 * jax.random.normal(jax.random.fold_in(_tk, 500 + 26), (1000, 16), jnp.float32)
        tbl_27 = 0.05 * jax.random.normal(jax.random.fold_in(_tk, 500 + 27), (1000, 16), jnp.float32)
        tbl_28 = 0.05 * jax.random.normal(jax.random.fold_in(_tk, 500 + 28), (1250, 16), jnp.float32)
        tbl_29 = 0.05 * jax.random.normal(jax.random.fold_in(_tk, 500 + 29), (1000, 16), jnp.float32)
        tbl_30 = 0.05 * jax.random.normal(jax.random.fold_in(_tk, 500 + 30), (125000, 16), jnp.float32)
        tbl_31 = 0.05 * jax.random.normal(jax.random.fold_in(_tk, 500 + 31), (1000, 16), jnp.float32)
        _rk = jax.random.fold_in(_tk, 7)
        W_top1 = 0.0693375 * jax.random.normal(jax.random.fold_in(_tk, 801), (208, 512), jnp.float32)
        W_top2 = 0.0441942 * jax.random.normal(jax.random.fold_in(_tk, 802), (512, 256), jnp.float32)
        W_top3 = 0.0625 * jax.random.normal(jax.random.fold_in(_tk, 803), (256, 1), jnp.float32)
        b_top1 = jnp.zeros((512,), jnp.float32)
        b_top2 = jnp.zeros((256,), jnp.float32)
        return (dense_ctx, ids, tbl_0, tbl_1, tbl_2, tbl_3, tbl_4, tbl_5, tbl_6, tbl_7, tbl_8, tbl_9, tbl_10, tbl_11, tbl_12, tbl_13, tbl_14, tbl_15, tbl_16, tbl_17, tbl_18, tbl_19, tbl_20, tbl_21, tbl_22, tbl_23, tbl_24, tbl_25, tbl_26, tbl_27, tbl_28, tbl_29, tbl_30, tbl_31, W_top1, b_top1, W_top2, b_top2, W_top3)
    dense_ctx, ids, tbl_0, tbl_1, tbl_2, tbl_3, tbl_4, tbl_5, tbl_6, tbl_7, tbl_8, tbl_9, tbl_10, tbl_11, tbl_12, tbl_13, tbl_14, tbl_15, tbl_16, tbl_17, tbl_18, tbl_19, tbl_20, tbl_21, tbl_22, tbl_23, tbl_24, tbl_25, tbl_26, tbl_27, tbl_28, tbl_29, tbl_30, tbl_31, W_top1, b_top1, W_top2, b_top2, W_top3 = _rec_inputs()

    def _L0_rec_setup():
        import jax, jax.numpy as jnp
        import numpy as np
        B, M, D = (2048, 32, 16)
        LAYERS = [64, 64, 64]
        key = jax.random.key(seed)
        ks = jax.random.split(key, 4)
        inp = {'embeddings': jax.random.normal(ks[0], (B, M, D), dtype=jnp.float32)}
        hk_1 = M
        for i, hk in enumerate(LAYERS):
            scale = (2.0 / (M * hk_1 + hk)) ** 0.5
            inp[f'W{i}'] = jax.random.normal(ks[i + 1], (M, hk_1, hk), dtype=jnp.float32) * scale
            hk_1 = hk
        return inp
    _L0_rec_all = _L0_rec_setup()
    _L0_rec_in = {k: v for k, v in _L0_rec_all.items() if k in ('W0', 'W1', 'W2')}
    del _L0_rec_all
    return {'dense_ctx': dense_ctx, 'ids': ids, 'tbl_0': tbl_0, 'tbl_1': tbl_1, 'tbl_2': tbl_2, 'tbl_3': tbl_3, 'tbl_4': tbl_4, 'tbl_5': tbl_5, 'tbl_6': tbl_6, 'tbl_7': tbl_7, 'tbl_8': tbl_8, 'tbl_9': tbl_9, 'tbl_10': tbl_10, 'tbl_11': tbl_11, 'tbl_12': tbl_12, 'tbl_13': tbl_13, 'tbl_14': tbl_14, 'tbl_15': tbl_15, 'tbl_16': tbl_16, 'tbl_17': tbl_17, 'tbl_18': tbl_18, 'tbl_19': tbl_19, 'tbl_20': tbl_20, 'tbl_21': tbl_21, 'tbl_22': tbl_22, 'tbl_23': tbl_23, 'tbl_24': tbl_24, 'tbl_25': tbl_25, 'tbl_26': tbl_26, 'tbl_27': tbl_27, 'tbl_28': tbl_28, 'tbl_29': tbl_29, 'tbl_30': tbl_30, 'tbl_31': tbl_31, 'W_top1': W_top1, 'b_top1': b_top1, 'W_top2': W_top2, 'b_top2': b_top2, 'W_top3': W_top3, 'L0_rec_W0': _L0_rec_in['W0'], 'L0_rec_W1': _L0_rec_in['W1'], 'L0_rec_W2': _L0_rec_in['W2']}

def reference(dense_ctx, ids, tbl_0, tbl_1, tbl_2, tbl_3, tbl_4, tbl_5, tbl_6, tbl_7, tbl_8, tbl_9, tbl_10, tbl_11, tbl_12, tbl_13, tbl_14, tbl_15, tbl_16, tbl_17, tbl_18, tbl_19, tbl_20, tbl_21, tbl_22, tbl_23, tbl_24, tbl_25, tbl_26, tbl_27, tbl_28, tbl_29, tbl_30, tbl_31, W_top1, b_top1, W_top2, b_top2, W_top3, L0_rec_W0, L0_rec_W1, L0_rec_W2):
    import jax
    import jax.numpy as jnp

    def _L0_rec_ref(embeddings, W0, W1, W2):
        import jax, jax.numpy as jnp
        import numpy as np
        B, M, D = (2048, 32, 16)
        LAYERS = [64, 64, 64]
        x0 = embeddings
        xk = x0
        outs = []
        for W in (W0, W1, W2):
            xk = jax.nn.relu(jnp.einsum('bmd,bhd,mhk->bkd', x0, xk, W))
            outs.append(jnp.sum(xk, axis=2))
        return jnp.concatenate(outs, axis=1)
    e = jnp.stack([tbl_0[ids[:, 0]], tbl_1[ids[:, 1]], tbl_2[ids[:, 2]], tbl_3[ids[:, 3]], tbl_4[ids[:, 4]], tbl_5[ids[:, 5]], tbl_6[ids[:, 6]], tbl_7[ids[:, 7]], tbl_8[ids[:, 8]], tbl_9[ids[:, 9]], tbl_10[ids[:, 10]], tbl_11[ids[:, 11]], tbl_12[ids[:, 12]], tbl_13[ids[:, 13]], tbl_14[ids[:, 14]], tbl_15[ids[:, 15]], tbl_16[ids[:, 16]], tbl_17[ids[:, 17]], tbl_18[ids[:, 18]], tbl_19[ids[:, 19]], tbl_20[ids[:, 20]], tbl_21[ids[:, 21]], tbl_22[ids[:, 22]], tbl_23[ids[:, 23]], tbl_24[ids[:, 24]], tbl_25[ids[:, 25]], tbl_26[ids[:, 26]], tbl_27[ids[:, 27]], tbl_28[ids[:, 28]], tbl_29[ids[:, 29]], tbl_30[ids[:, 30]], tbl_31[ids[:, 31]]], axis=1)
    z = _L0_rec_ref(e, L0_rec_W0, L0_rec_W1, L0_rec_W2)
    z = z.reshape(z.shape[0], -1)
    h = jnp.concatenate([z, dense_ctx], axis=1)
    h = jnp.maximum(h @ W_top1 + b_top1, 0.0)
    h = jnp.maximum(h @ W_top2 + b_top2, 0.0)
    y = h @ W_top3
    return y

_drawn_inputs = setup_inputs


def setup_inputs(seed=0):
    import zlib

    import numpy as np

    out = dict(_drawn_inputs(seed))
    spreads = {'b_top1': (0.0, 2.0), 'b_top2': (0.0, 0.8)}
    factors = {'tbl_0': 8.0,
     'tbl_1': 8.0,
     'tbl_2': 8.0,
     'tbl_3': 8.0,
     'tbl_4': 8.0,
     'tbl_5': 8.0,
     'tbl_6': 8.0,
     'tbl_7': 8.0,
     'tbl_8': 8.0,
     'tbl_9': 8.0,
     'tbl_10': 8.0,
     'tbl_11': 8.0,
     'tbl_12': 8.0,
     'tbl_13': 8.0,
     'tbl_14': 8.0,
     'tbl_15': 8.0,
     'tbl_16': 8.0,
     'tbl_17': 8.0,
     'tbl_18': 8.0,
     'tbl_19': 8.0,
     'tbl_20': 8.0,
     'tbl_21': 8.0,
     'tbl_22': 8.0,
     'tbl_23': 8.0,
     'tbl_24': 8.0,
     'tbl_25': 8.0,
     'tbl_26': 8.0,
     'tbl_27': 8.0,
     'tbl_28': 8.0,
     'tbl_29': 8.0,
     'tbl_30': 8.0,
     'tbl_31': 8.0,
     'L0_rec_W0': 3.589,
     'L0_rec_W1': 8.0,
     'L0_rec_W2': 8.0,
     'dense_ctx': 7.431}
    for name, (base, spread) in spreads.items():
        noise = np.random.default_rng([zlib.crc32(name.encode()), seed]).standard_normal(out[name].shape)
        drawn = base * np.exp(spread * noise) if base else spread * noise
        out[name] = jnp.asarray(drawn.astype(out[name].dtype))
    for name, factor in factors.items():
        out[name] = (out[name] * factor).astype(out[name].dtype)
    return out
```

```python
import concourse.bass as bass
from concourse import mybir
from contextlib import ExitStack

BATCH, FIELDS, DIM, HID = 2048, 32, 16, 64
P = 128
BLOCK = P
BLOCKS = BATCH // BLOCK
BANK = 512
GROUP_D = BANK // BLOCK
GROUPS = DIM // GROUP_D
STEP = 2 * BANK
STEPS_PER_BLOCK = GROUPS // 2
COLS = DIM * BLOCK
FIELD_GROUP = P // DIM
FIELD_GROUPS = FIELDS // FIELD_GROUP
SCRATCH_DMAS = 2
DUP = 2 * FIELDS

DELTAS = [(1, 2), (2, 4), (9, 2), (0, 4), (16, 4)]
SYMMETRIC = 3
T0 = len(DELTAS)
T1 = FIELDS // 2
LOAD = 4
LOADS = T1 // LOAD
assert LOAD == 4

POOL_EVERY = 4
POOL_TILES = [j for j in range(T1) if j % POOL_EVERY == POOL_EVERY - 1]
DVE_TILES = [j for j in range(T1) if j % POOL_EVERY != POOL_EVERY - 1]
NV, NP = len(DVE_TILES), len(POOL_TILES)
RING_V, RING_0, RING_P = 6, 2, NP

EARLY = 20
LATE = FIELDS - EARLY

TOP1, TOP2 = 512, 256
Z_COLS = 3 * HID
CHUNK = BANK


def odd_tiles(j):
    return (j + 1) // 2


def build(nc, dense_t, ids, tables, w0a, w0b, w1, w2, w_top1, b_top1, w_top2, b_top2, w_top3, out):
    F32, I32 = mybir.dt.float32, mybir.dt.int32
    ALU, ACT, AX = mybir.AluOpType, mybir.ActivationFunctionType, mybir.AxisListType

    scratch = nc.dram_tensor("x0_rows", (BLOCKS, DUP, COLS), F32, kind="Internal")

    def x0_rows(block, row, column, pattern):
        return bass.AP(scratch, block * (DUP * COLS) + (row * COLS + column), pattern)

    ctx = ExitStack()
    with ctx:
        def sb(name, shape, dt=F32):
            return ctx.enter_context(nc.sbuf_tensor(name, shape, dt))

        def pb(name, shape, dt=F32):
            return ctx.enter_context(nc.psum_tensor(name, shape, dt))

        def sem(name):
            return ctx.enter_context(nc.semaphore(name))

        ident = sb("ident", [P, P])
        fold = sb("fold", [P, HID])
        w0 = sb("w0", [P, T0, HID])
        w0_mirror = sb("w0_mirror", [P, SYMMETRIC, HID])
        wk = [sb("w1_sb", [P, T1, HID]), sb("w2_sb", [P, T1, HID])]
        wt1 = sb("wt1", [P, 2, TOP1])
        wt2 = sb("wt2", [P, TOP1 // P, TOP2])
        wt3 = sb("wt3", [P, TOP2 // P, 1])
        bt1 = sb("bt1", [P, TOP1 // P])
        bt2 = sb("bt2", [P, TOP2 // P])

        idx_first = sb("idx_first", [P, FIELDS], I32)
        idx_early = sb("idx_early", [P, EARLY], I32)
        idx_late = sb("idx_late", [P, LATE], I32)
        emb = sb("emb", [P, FIELDS, DIM])
        x0t = sb("x0t", [P, FIELD_GROUPS, BLOCK])

        x0_quad = sb("x0_quad", [P, STEP])
        x0_rot = sb("x0_rot", [P, T0, STEP])
        spread = sb("spread", [P, T1, STEP])
        xs = [sb("x1_sb", [P, STEP]), sb("x2_sb", [P, STEP])]
        z0 = sb("z0", [P, RING_0, STEP])
        zv = sb("zv", [P, RING_V, STEP])
        zp = sb("zp", [P, RING_P, STEP])
        act_out = [sb(f"act_out{n}", [P, STEPS_PER_BLOCK * GROUP_D, BLOCK]) for n in range(3)]
        pooled = sb("pooled", [P, 3, BATCH])

        top_z = spread[:, 0:1, :].rearrange("p a (t n) -> p (a t) n", t=2)
        top_h1 = spread[:, 1:3, :].rearrange("p a (t n) -> p (a t) n", t=2)
        top_h2 = spread[:, 3:4, :].rearrange("p a (t n) -> p (a t) n", t=2)
        top_y = spread[0:1, 4:6, :].rearrange("p a n -> p (a n)")
        dense = spread[:, 6:8, :].rearrange("p a n -> p (a n)")

        acc = [pb("acc0", [P, BANK]), pb("acc1", [P, BANK])]
        xp = [pb("x1_ps", [P, STEP]), pb("x2_ps", [P, STEP])]
        pt = pb("pt", [P, FIELD_GROUPS, BLOCK])
        top_ps = pb("top_ps", [P, BANK])

        w_in = sem("w_in")
        idx_first_in, idx_early_in, idx_late_in = sem("idx_first_in"), sem("idx_early_in"), sem("idx_late_in")
        first_gathered, early_gathered, late_gathered = sem("first_gathered"), sem("early_gathered"), sem("late_gathered")
        scratch_written = sem("scratch_written")
        quad_in = sem("quad_in")
        rot_in = [sem(f"rot_in{t}") for t in range(T0)]
        full_in = [sem(f"full_in{g}") for g in range(LOADS)]
        half_in = [sem(f"half_in{g}") for g in range(LOADS)]
        dense_in = sem("dense_in")
        out_written = sem("out_written")
        ident_ready, fold_ready, w0_ready = sem("ident_ready"), sem("fold_ready"), sem("w0_ready")
        transposed, x0t_ready = sem("transposed"), sem("x0t_ready")
        spread_ready = sem("spread_ready")
        z0_ready, zv_ready, zp_ready = sem("z0_ready"), sem("zv_ready"), sem("zp_ready")
        z0_used, zv_used, zp_used = sem("z0_used"), sem("zv_used"), sem("zp_used")
        xp_ready = [sem("x1_ps_ready"), sem("x2_ps_ready")]
        xs_ready = [sem("x1_sb_ready"), sem("x2_sb_ready")]
        evacuated = sem("evacuated")
        pooled_ready = [sem(f"pooled_ready{n}") for n in range(3)]
        fold_done, top_z_ready = sem("fold_done"), sem("top_z_ready")
        h1_done, h1_ready = sem("h1_done"), sem("h1_ready")
        h2_done, h2_ready = sem("h2_done"), sem("h2_ready")
        y_done, y_ready = sem("y_done"), sem("y_ready")

        LAST = BLOCKS - 1

        block = ctx.enter_context(nc.Block())

        @block.sync
        def _(sp):
            def load_operands0(b, h, step):
                sp.wait_ge(z0_ready, step * T0)
                sp.dma_start(x0_quad[:, :], x0_rows(b, 0, h * STEP, [[COLS, FIELDS], [0, 4], [1, STEP]])
                             ).then_inc(quad_in, 16)
                for t, (first, by) in enumerate(DELTAS):
                    sp.dma_start(x0_rot[:, t, :],
                                 x0_rows(b, first, h * STEP, [[COLS, FIELDS], [by * COLS, 4], [1, STEP]])
                                 ).then_inc(rot_in[t], 16)

            def load_spread(b, h, g):
                for odd in range(2):
                    rows = HID // 2 if odd else HID
                    for field in range(2):
                        j = LOAD * g + odd
                        sp.dma_start(spread[HID * field:HID * field + rows, j:j + LOAD - 1:2, :],
                                     x0_rows(b, 2 * j + field, h * STEP,
                                             [[0, rows], [4 * COLS, LOAD // 2], [1, STEP]])
                                     ).then_inc((half_in if odd else full_in)[g], 16)

            def write_scratch(b):
                for half in range(2):
                    sp.dma_start(x0_rows(b, half * FIELDS, 0, [[BLOCK, P], [FIELD_GROUP * COLS, FIELD_GROUPS], [1, BLOCK]]),
                                 x0t[:, :, :]).then_inc(scratch_written, 16)

            ids_b = ids.rearrange("(n p) f -> n p f", p=BLOCK)
            sp.dma_start(idx_first[:, :], ids_b[0, :, :]).then_inc(idx_first_in, 16)
            sp.dma_start(idx_early[:, :], ids_b[1, :, 0:EARLY]).then_inc(idx_early_in, 16)
            sp.dma_start(idx_late[:, :], ids_b[1, :, EARLY:FIELDS]).then_inc(idx_late_in, 16)
            for dst, src in ((w0[:, :, :], w0a), (w0_mirror[:, :, :], w0b), (wk[0][:, :, :], w1),
                             (wk[1][:, :, :], w2), (wt1[:, 0, :], w_top1[0:P, :]),
                             (wt1[0:Z_COLS + DIM - P, 1, :], w_top1[P:Z_COLS + DIM, :]),
                             (wt2[:, :, :], w_top2.rearrange("(t p) n -> p t n", p=P)),
                             (wt3[:, 0, :], w_top3[0:P, :]), (wt3[:, 1, :], w_top3[P:2 * P, :]),
                             (bt1[:, :], b_top1), (bt2[:, :], b_top2)):
                sp.dma_start(dst, src).then_inc(w_in, 16)
            sp.wait_ge(x0t_ready, 1)
            write_scratch(0)
            sp.wait_ge(scratch_written, 16 * SCRATCH_DMAS)
            load_operands0(0, 0, 0)
            for g in range(LOADS):
                load_spread(0, 0, g)
            load_operands0(0, 1, 1)

            def half(i, h, last=False, more=True):
                s = 2 * i + h
                nb, nh = (i, 1) if h == 0 else (i + 1, 0)
                if h == 1 and not last:
                    load_operands0(i + 1, 1, 2 * i + 3)
                if not (last and h == 1):
                    for g in range(LOADS):
                        sp.wait_ge(zp_used, NP * (2 * s + 1) + (g + 1))
                        load_spread(nb, nh, g)
                        if h == 0 and g == 0 and more:
                            sp.wait_ge(early_gathered, 16 * EARLY * (i + 1))
                            sp.dma_start(idx_early[:, :], ids_b[i + 2, :, 0:EARLY]).then_inc(idx_early_in, 16)
                if h == 0 and not last:
                    sp.wait_ge(x0t_ready, i + 2)
                    write_scratch(i + 1)
                    if more:
                        sp.wait_ge(late_gathered, 16 * LATE * (i + 1))
                        sp.dma_start(idx_late[:, :], ids_b[i + 2, :, EARLY:FIELDS]).then_inc(idx_late_in, 16)
                    sp.wait_ge(scratch_written, 16 * SCRATCH_DMAS * (i + 2))
                    load_operands0(i + 1, 0, 2 * i + 2)

            with sp.Fori(0, LAST - 1) as i:
                half(i, 0)
                half(i, 1)
            half(LAST - 1, 0, more=False)
            half(LAST - 1, 1, more=False)
            half(LAST, 0, last=True, more=False)
            sp.wait_ge(zp_used, NP * 4 * BLOCKS)
            sp.dma_start(dense[Z_COLS - P:Z_COLS - P + DIM, :], dense_t).then_inc(dense_in, 16)
            for c in range(BATCH // CHUNK):
                sp.wait_ge(y_ready, c + 1)
                sp.dma_start(out[:, c * CHUNK:(c + 1) * CHUNK], top_y[:, c * CHUNK:(c + 1) * CHUNK]
                             ).then_inc(out_written, 16)
            sp.wait_ge(out_written, 16 * (BATCH // CHUNK))

        @block.gpsimd
        def _(pool):
            def gather(f, idx, gathered):
                nc.gpsimd.indirect_dma_start(emb[:, f, :], None, tables[f],
                                             bass.IndirectOffsetOnAxis(ap=idx, axis=0)).then_inc(gathered, 16)

            def early(f):
                gather(f, idx_early[:, f:f + 1], early_gathered)

            def late(f):
                gather(EARLY + f, idx_late[:, f:f + 1], late_gathered)

            def product(layer, run, k):
                nc.gpsimd.tensor_tensor(out=zp[:, k, :], in0=spread[:, POOL_TILES[k], :], in1=xs[layer - 1][:, :],
                                        op=ALU.mult).then_inc(zp_ready, 1)

            nc.gpsimd.memset(ident[:, :], 0.0).then_inc(ident_ready, 1)
            nc.gpsimd.memset(fold[:, :], 0.0).then_inc(fold_ready, 1)
            pool.wait_ge(ident_ready, 1)
            nc.gpsimd.affine_select(out=ident[:, :], in_=ident[:, :], compare_op=ALU.not_equal, fill=1.0, base=0,
                                    pattern=[[-1, P]], channel_multiplier=1).then_inc(ident_ready, 1)
            pool.wait_ge(idx_first_in, 16)
            for f in range(FIELDS):
                gather(f, idx_first[:, f:f + 1], first_gathered)
            for n, base in enumerate((0, -HID)):
                pool.wait_ge(fold_ready, n + 1)
                nc.gpsimd.affine_select(out=fold[:, :], in_=fold[:, :], compare_op=ALU.not_equal, fill=1.0, base=base,
                                        pattern=[[-1, HID]], channel_multiplier=1).then_inc(fold_ready, 1)
            pool.wait_ge(idx_early_in, 16)
            pool.wait_ge(idx_late_in, 16)
            pool.wait_ge(transposed, 1)
            for f in range(EARLY - NP):
                early(f)
            pool.wait_ge(xs_ready[0], 1)
            for k in range(NP):
                pool.wait_ge(spread_ready, odd_tiles(POOL_TILES[k]))
                product(1, 0, k)
                early(EARLY - NP + k)

            def half(i, h, last=False, more=True):
                s = 2 * i + h
                if h == 0 and not last:
                    for f in range(LATE - NP):
                        late(f)
                if h == 1 and more:
                    for f in range(NP, EARLY - 2 * NP):
                        early(f)
                for k in range(NP):
                    if h == 0 and not last:
                        late(LATE - NP + k)
                    if h == 1 and more:
                        early(EARLY - 2 * NP + k)
                    if k == 0:
                        pool.wait_ge(xs_ready[1], s + 1)
                    pool.wait_ge(zp_used, NP * (2 * s) + k + 1)
                    product(2, 2 * s + 1, k)
                if last and h == 1:
                    return
                pool.wait_ge(xs_ready[0], s + 2)
                for k in range(NP):
                    pool.wait_ge(zp_used, NP * (2 * s + 1) + k + 1)
                    if h == 0 and more and k == 1:
                        pool.wait_ge(transposed, i + 2)
                        pool.wait_ge(idx_early_in, 16 * (i + 2))
                    if h == 1 and more and k == NP - 1:
                        pool.wait_ge(idx_late_in, 16 * (i + 2))
                    pool.wait_ge(spread_ready, T1 // 2 * (s + 1) + odd_tiles(POOL_TILES[k]))
                    product(1, 2 * s + 2, k)
                    if h == 0 and more and k > 0:
                        if k == 1:
                            early(0)
                        early(k)
                    if h == 1 and more:
                        early(EARLY - NP + k)

            with pool.Fori(0, LAST - 1) as i:
                half(i, 0)
                half(i, 1)
            half(LAST - 1, 0, more=False)
            half(LAST - 1, 1, more=False)
            half(LAST, 0, last=True, more=False)
            half(LAST, 1, last=True, more=False)

        @block.vector
        def _(dve):
            dve.wait_ge(w_in, 16 * 11)
            nc.vector.tensor_tensor(out=w0[:, 0:SYMMETRIC, :], in0=w0[:, 0:SYMMETRIC, :], in1=w0_mirror[:, :, :],
                                    op=ALU.add).then_inc(w0_ready, 1)

            def layer0(step, parity):
                dve.wait_ge(quad_in, 16 * (step + 1))
                for t in range(T0):
                    dve.wait_ge(rot_in[t], 16 * (step + 1))
                    if not (isinstance(step, int) and step * T0 + t < RING_0):
                        dve.wait_ge(z0_used, step * T0 + (t + 1 - RING_0))
                    nc.vector.tensor_tensor(out=z0[:, (parity * T0 + t) % RING_0, :], in0=x0_quad[:, :],
                                            in1=x0_rot[:, t, :], op=ALU.mult).then_inc(z0_ready, 1)

            def layer(number, step, run):
                dve.wait_ge(xp_ready[number - 1], step + 1)
                for k, j in enumerate(DVE_TILES):
                    if not (isinstance(run, int) and run * NV + k < RING_V):
                        dve.wait_ge(zv_used, run * NV + (k + 1 - RING_V))
                    if number == 1 and j % 2:
                        dve.wait_ge(spread_ready, step * (T1 // 2) + odd_tiles(j))
                    elif number == 1:
                        dve.wait_ge(full_in[j // LOAD], 32 * (step + 1))
                    nc.vector.tensor_tensor(out=zv[:, k % RING_V, :], in0=xp[number - 1][:, :], in1=spread[:, j, :],
                                            op=ALU.mult).then_inc(zv_ready, 1)

            def pool_dims(n, i, runs=None):
                dve.wait_ge(evacuated, runs or 6 * i + (3, 5, 7)[n])
                nc.vector.tensor_reduce(out=pooled[:, n, bass.ds(i * BLOCK, BLOCK)],
                                        in_=act_out[n][:, :, :].rearrange("p d b -> p b d"),
                                        axis=AX.X, op=ALU.add).then_inc(pooled_ready[n], 1)

            layer0(0, 0)
            layer(1, 0, 0)

            def body(i, last=False):
                layer0(2 * i + 1, 1)
                layer(2, 2 * i, 4 * i + 1)
                layer(1, 2 * i + 1, 4 * i + 2)
                pool_dims(0, i)
                if not last:
                    layer0(2 * i + 2, 0)
                layer(2, 2 * i + 1, 4 * i + 3)
                pool_dims(1, i)
                if not last:
                    layer(1, 2 * i + 2, 4 * i + 4)
                pool_dims(2, i, 6 * BLOCKS if last else None)

            with dve.Fori(0, LAST) as i:
                body(i)
            body(LAST, last=True)

        @block.scalar
        def _(act):
            def copy_x0t(b):
                act.wait_ge(transposed, b + 1)
                if not (isinstance(b, int) and b == 0):
                    act.wait_ge(scratch_written, 16 * SCRATCH_DMAS * b)
                nc.scalar.activation(x0t[:, :, :], pt[:, :, :], ACT.Copy).then_inc(x0t_ready, 1)

            def spread_halves(step, g):
                act.wait_ge(half_in[g], 32 * (step + 1))
                for j in range(LOAD * g + 1, LOAD * g + LOAD, 2):
                    for q in (0, HID):
                        ins = nc.scalar.activation(spread[q + 32:q + 64, j, :], spread[q:q + 32, j, :], ACT.Copy)
                    ins.then_inc(spread_ready, 1)

            def evacuate(n, bank, consumed, count, h):
                act.wait_ge(consumed, count)
                if n < 2:
                    for operand, ready in ((xp[n], xp_ready[n]), (xs[n], xs_ready[n])):
                        for ab in range(2):
                            for dst in (0, HID):
                                ins = nc.scalar.activation(operand[dst:dst + HID, ab * BANK:(ab + 1) * BANK],
                                                           acc[bank][HID * ab:HID * ab + HID, :], ACT.Relu)
                        ins.then_inc(ready, 1)
                nc.scalar.activation(act_out[n][:, h * GROUP_D:(h + 1) * GROUP_D, :],
                                     acc[bank][:, :].rearrange("p (d b) -> p d b", d=GROUP_D),
                                     ACT.Relu).then_inc(evacuated, 1)

            copy_x0t(0)
            spread_halves(0, 0)
            evacuate(0, 0, z0_used, T0, 0)
            for g in range(1, LOADS):
                spread_halves(0, g)

            def half(i, h, last=False):
                s = 2 * i + h
                end = last and h == 1
                evacuate(1, (1 + 3 * h) % 2, zp_used, NP * (2 * s + 1), h)
                if not end:
                    evacuate(0, (2 + 3 * h) % 2, z0_used, T0 * (s + 2), 1 - h)
                    for g in range(LOADS - 1):
                        spread_halves(s + 1, g)
                    if h == 0 and not last:
                        copy_x0t(i + 1)
                evacuate(2, (3 + 3 * h) % 2, zp_used, NP * (2 * s + 2), h)
                if not end:
                    spread_halves(s + 1, LOADS - 1)

            with act.Fori(0, LAST) as i:
                half(i, 0)
                half(i, 1)
            half(LAST, 0, last=True)
            half(LAST, 1, last=True)

            act.wait_ge(zp_used, NP * 4 * BLOCKS)
            act.wait_ge(dense_in, 16)
            for c in range(BATCH // CHUNK):
                cs = slice(c * CHUNK, (c + 1) * CHUNK)
                rows = Z_COLS - P
                act.wait_ge(fold_done, c + 1)
                if c > 0:
                    act.wait_ge(h1_done, c * (TOP1 // P))
                nc.scalar.activation(top_z[:, 0, :], acc[0][:, :], ACT.Copy)
                nc.scalar.activation(top_z[0:rows, 1, :], acc[1][0:rows, :], ACT.Copy)
                nc.scalar.activation(top_z[rows:rows + DIM, 1, :], dense[rows:rows + DIM, cs], ACT.Copy
                                     ).then_inc(top_z_ready, 1)
                for t in range(TOP1 // P):
                    act.wait_ge(h1_done, c * (TOP1 // P) + t + 1)
                    if c > 0 and t == 0:
                        act.wait_ge(h2_done, c * (TOP2 // P))
                    nc.scalar.activation(top_h1[:, t, :], xp[t // 2][:, (t % 2) * BANK:(t % 2 + 1) * BANK],
                                         ACT.Relu, bias=bt1[:, t:t + 1]).then_inc(h1_ready, 1)
                for t in range(TOP2 // P):
                    act.wait_ge(h2_done, c * (TOP2 // P) + t + 1)
                    if c > 0 and t == 0:
                        act.wait_ge(y_done, c)
                    nc.scalar.activation(top_h2[:, t, :], [top_ps, pt][t][:, :] if t == 0 else
                                         pt[:, :, :].rearrange("p g b -> p (g b)"),
                                         ACT.Relu, bias=bt2[:, t:t + 1]).then_inc(h2_ready, 1)
                act.wait_ge(y_done, c + 1)
                nc.scalar.activation(top_y[0:1, cs], top_ps[0:1, :], ACT.Copy).then_inc(y_ready, 1)

        @block.tensor
        def _(pe):
            def transpose_block(b):
                by_group = emb[:, :, :].rearrange("p (g m) d -> p g (m d)", g=FIELD_GROUPS)
                if not (isinstance(b, int) and b == 0):
                    pe.wait_ge(early_gathered, 16 * EARLY * b)
                    pe.wait_ge(late_gathered, 16 * LATE * b)
                    pe.wait_ge(x0t_ready, b)
                for g in range(FIELD_GROUPS):
                    ins = nc.tensor.transpose(pt[:, g, :], by_group[:, g, :], ident[:, :])
                ins.then_inc(transposed, 1)

            def contract(bank, weights, z, first, last, used):
                for ab in range(2):
                    ins = nc.tensor.matmul(acc[bank][64 * ab:64 * ab + 64, :], weights,
                                           z[:, ab * BANK:(ab + 1) * BANK], start=first, stop=last)
                ins.then_inc(used, 1)

            def layer0(step, parity, bank):
                for t in range(T0):
                    pe.wait_ge(z0_ready, step * T0 + (t + 1))
                    contract(bank, w0[:, t, :], z0[:, (parity * T0 + t) % RING_0, :], t == 0, t == T0 - 1, z0_used)

            def layer(number, run, bank, between=None):
                k_v = k_p = 0
                for j in range(T1):
                    if j in POOL_TILES:
                        pe.wait_ge(zp_ready, run * NP + (k_p + 1))
                        contract(bank, wk[number - 1][:, j, :], zp[:, k_p, :], j == 0, j == T1 - 1, zp_used)
                        k_p += 1
                    else:
                        pe.wait_ge(zv_ready, run * NV + (k_v + 1))
                        contract(bank, wk[number - 1][:, j, :], zv[:, k_v % RING_V, :], j == 0, j == T1 - 1, zv_used)
                        k_v += 1
                    if j == 1 and between is not None:
                        transpose_block(between)

            pe.wait_ge(ident_ready, 2)
            pe.wait_ge(first_gathered, 16 * FIELDS)
            transpose_block(0)
            pe.wait_ge(w0_ready, 1)
            layer0(0, 0, 0)
            layer(1, 0, 1)

            def half(i, h, last=False):
                s = 2 * i + h
                end = last and h == 1
                if not end:
                    pe.wait_ge(evacuated, 3 * s + 1)
                    layer0(s + 1, 1 - h, (2 + 3 * h) % 2)
                pe.wait_ge(evacuated, 3 * s + 2)
                layer(2, 2 * s + 1, (3 + 3 * h) % 2)
                if not end:
                    pe.wait_ge(evacuated, 3 * s + 3)
                    layer(1, 2 * s + 2, (4 + 3 * h) % 2, i + 1 if h == 0 and not last else None)

            with pe.Fori(0, LAST) as i:
                half(i, 0)
                half(i, 1)
            half(LAST, 0, last=True)
            half(LAST, 1, last=True)

            pe.wait_ge(evacuated, 6 * BLOCKS)
            pe.wait_ge(fold_ready, 3)
            for n in range(3):
                pe.wait_ge(pooled_ready[n], BLOCKS)
            rows = Z_COLS + DIM - P
            for c in range(BATCH // CHUNK):
                cs = slice(c * CHUNK, (c + 1) * CHUNK)
                if c > 0:
                    pe.wait_ge(top_z_ready, c)
                nc.tensor.matmul(acc[0][0:HID, :], fold[:, :], pooled[:, 0, cs], start=True, stop=True)
                nc.tensor.matmul(acc[0][HID:P, :], fold[:, :], pooled[:, 1, cs], start=True, stop=True)
                nc.tensor.matmul(acc[1][0:HID, :], fold[:, :], pooled[:, 2, cs], start=True, stop=True
                                 ).then_inc(fold_done, 1)
                pe.wait_ge(top_z_ready, c + 1)
                for t in range(TOP1 // P):
                    if c > 0:
                        pe.wait_ge(h1_ready, (c - 1) * (TOP1 // P) + t + 1)
                    dst = xp[t // 2][:, (t % 2) * BANK:(t % 2 + 1) * BANK]
                    nc.tensor.matmul(dst, wt1[:, 0, t * P:(t + 1) * P], top_z[:, 0, :], start=True, stop=False)
                    nc.tensor.matmul(dst, wt1[0:rows, 1, t * P:(t + 1) * P], top_z[0:rows, 1, :],
                                     start=False, stop=True).then_inc(h1_done, 1)
                if c > 0:
                    pe.wait_ge(y_ready, c)
                for u in range(TOP2 // P):
                    dst = top_ps[:, :] if u == 0 else pt[:, :, :].rearrange("p g b -> p (g b)")
                    for t in range(TOP1 // P):
                        if u == 0:
                            pe.wait_ge(h1_ready, c * (TOP1 // P) + t + 1)
                        ins = nc.tensor.matmul(dst, wt2[:, t, u * P:(u + 1) * P], top_h1[:, t, :],
                                               start=(t == 0), stop=(t == TOP1 // P - 1))
                    ins.then_inc(h2_done, 1)
                for u in range(TOP2 // P):
                    pe.wait_ge(h2_ready, c * (TOP2 // P) + u + 1)
                    ins = nc.tensor.matmul(top_ps[0:1, :], wt3[:, u, :], top_h2[:, u, :],
                                           start=(u == 0), stop=(u == TOP2 // P - 1))
                ins.then_inc(y_done, 1)


def kernel(**inputs):
    import numpy as np
    import concourse.bacc as bacc
    from concourse.bass_utils import run_bass_kernel_spmd

    def plain(name):
        return np.ascontiguousarray(inputs[name])

    W0 = plain("L0_rec_W0")
    m = np.arange(FIELDS)[:, None, None]
    delta = np.array([[first + by * i for first, by in DELTAS] for i in range(4)])[None, :, :]
    other = (m + delta) % FIELDS
    arrays = {"dense_t": np.ascontiguousarray(plain("dense_ctx").T), "ids": plain("ids")}
    for f in range(FIELDS):
        arrays[f"tbl_{f}"] = plain(f"tbl_{f}")
    arrays["w0a"] = np.ascontiguousarray(W0[m, other].reshape(P, T0, HID))
    arrays["w0b"] = np.ascontiguousarray(W0[other, m][:, :, :SYMMETRIC].reshape(P, SYMMETRIC, HID))
    for n in (1, 2):
        w = plain(f"L0_rec_W{n}").reshape(T1, P, HID)
        arrays[f"w{n}"] = np.ascontiguousarray(w.transpose(1, 0, 2))
    arrays["w_top1"] = plain("W_top1")
    arrays["b_top1"] = np.ascontiguousarray(plain("b_top1").reshape(TOP1 // P, P).T)
    arrays["w_top2"] = plain("W_top2")
    arrays["b_top2"] = np.ascontiguousarray(plain("b_top2").reshape(TOP2 // P, P).T)
    arrays["w_top3"] = plain("W_top3")

    nc = bacc.Bacc("TRN2", target_bir_lowering=False, num_devices=1)
    aps = {name: nc.dram_tensor(name, a.shape, mybir.dt.from_np(a.dtype), kind="ExternalInput").ap()
           for name, a in arrays.items()}
    out = nc.dram_tensor("out", (1, BATCH), mybir.dt.float32, kind="ExternalOutput").ap()
    build(nc, aps["dense_t"], aps["ids"], [aps[f"tbl_{f}"] for f in range(FIELDS)], aps["w0a"], aps["w0b"],
          aps["w1"], aps["w2"], aps["w_top1"], aps["b_top1"], aps["w_top2"], aps["b_top2"], aps["w_top3"], out)
    r = run_bass_kernel_spmd(nc, [arrays], core_ids=[0])
    return r.results[0]["out"].reshape(BATCH, 1)
```

```python
import concourse.bass as bass
from concourse import mybir
from contextlib import ExitStack

BATCH, FIELDS, DIM, HID = 2048, 32, 16, 64
P = 128
BLOCK = P
BLOCKS = BATCH // BLOCK
BANK = 512
GROUP_D = BANK // BLOCK
GROUPS = DIM // GROUP_D
STEP = 2 * BANK
STEPS_PER_BLOCK = GROUPS // 2
COLS = DIM * BLOCK
FIELD_GROUP = P // DIM
FIELD_GROUPS = FIELDS // FIELD_GROUP
SCRATCH_DMAS = 2
DUP = 2 * FIELDS

DELTAS = [(1, 2), (2, 4), (9, 2), (0, 4), (16, 4)]
SYMMETRIC = 3
T0 = len(DELTAS)
T1 = FIELDS // 2
LOAD = 4
LOADS = T1 // LOAD
assert LOAD == 4

POOL_EVERY = 4
POOL_TILES = [j for j in range(T1) if j % POOL_EVERY == POOL_EVERY - 1]
DVE_TILES = [j for j in range(T1) if j % POOL_EVERY != POOL_EVERY - 1]
NV, NP = len(DVE_TILES), len(POOL_TILES)
assert LOAD == POOL_EVERY
RING_V, RING_0, RING_P = 3, 2, NP
TWICE = T1 // 2

PART = FIELDS // 2
TOP1, TOP2 = 512, 256
Z_COLS = 3 * HID
REST = Z_COLS - P


def odd_tiles(j):
    return (j + 1) // 2


def build(nc, dense_t, ids, tables, w0a, w0b, w1, w2, w_top1, b_top1, w_top2, b_top2, w_top3, out):
    F32, I32 = mybir.dt.float32, mybir.dt.int32
    ALU, ACT, AX = mybir.AluOpType, mybir.ActivationFunctionType, mybir.AxisListType

    scratch = nc.dram_tensor("x0_rows", (BLOCKS, DUP, COLS), F32, kind="Internal")

    def x0_rows(block, row, column, pattern):
        return bass.AP(scratch, block * (DUP * COLS) + (row * COLS + column), pattern)

    ctx = ExitStack()
    with ctx:
        def sb(name, shape, dt=F32):
            return ctx.enter_context(nc.sbuf_tensor(name, shape, dt))

        def pb(name, shape, dt=F32):
            return ctx.enter_context(nc.psum_tensor(name, shape, dt))

        def sem(name):
            return ctx.enter_context(nc.semaphore(name))

        ident = sb("ident", [P, P])
        fold = sb("fold", [P, HID])
        w0 = sb("w0", [P, T0, HID])
        w0_mirror = sb("w0_mirror", [P, SYMMETRIC, HID])
        wk = [sb("w1_sb", [P, T1, HID]), sb("w2_sb", [P, T1, HID])]
        wt1 = sb("wt1", [P, 2, TOP1])
        wt2 = sb("wt2", [P, TOP1 // P, TOP2])
        wt3 = sb("wt3", [P, TOP2 // P, 1])
        bt1 = sb("bt1", [P, TOP1 // P])
        bt2 = sb("bt2", [P, TOP2 // P])

        idx_first = sb("idx_first", [P, FIELDS], I32)
        idx = [sb("idx_a", [P, PART], I32), sb("idx_b", [P, PART], I32)]
        emb = sb("emb", [P, FIELDS, DIM])
        x0t = sb("x0t", [P, FIELD_GROUPS, BLOCK])

        x0_quad = sb("x0_quad", [P, STEP])
        x0_rot = sb("x0_rot", [P, T0, STEP])
        spread_twice = [sb("spread_even", [P, TWICE, STEP]), sb("spread_odd", [P, TWICE, STEP])]
        spread_once = sb("spread_once", [P, T1 - TWICE, STEP])

        def spread(j, parity):
            return (spread_twice[parity], j) if j < TWICE else (spread_once, j - TWICE)

        xs = [sb("x1_sb", [P, STEP]), sb("x2_sb", [P, STEP])]
        z0 = sb("z0", [P, RING_0, STEP])
        zv = sb("zv", [P, RING_V, STEP])
        zp = sb("zp", [P, RING_P, STEP])
        act_out = [sb(f"act_out{n}", [P, STEPS_PER_BLOCK * GROUP_D, BLOCK]) for n in range(3)]
        pooled = sb("pooled", [P, 3, BLOCK])
        top_z = sb("top_z", [P, 2, BLOCK])
        top_h1 = sb("top_h1", [P, TOP1 // P, BLOCK])
        top_h2 = sb("top_h2", [P, TOP2 // P, BLOCK])
        top_y = sb("top_y", [1, BLOCK])

        acc = [pb("acc0", [P, BANK]), pb("acc1", [P, BANK])]
        xp = [pb("x1_ps", [P, STEP]), pb("x2_ps", [P, STEP])]
        pt = pb("pt", [P, FIELD_GROUPS, BLOCK])
        top_ps = pb("top_ps", [P, TOP1 // P, BLOCK])

        w_in = sem("w_in")
        idx_first_in, idx_in = sem("idx_first_in"), [sem("idx_a_in"), sem("idx_b_in")]
        first_gathered, gathered = sem("first_gathered"), [sem("gathered_a"), sem("gathered_b")]
        scratch_written = sem("scratch_written")
        quad_in = sem("quad_in")
        rot_in = [sem(f"rot_in{t}") for t in range(T0)]
        full_in = [[sem(f"full_in{g}_{'even' if h == 0 else 'odd'}") for h in range(2)] if LOAD * g < TWICE
                   else [sem(f"full_in{g}")] * 2 for g in range(LOADS)]
        half_in = [[sem(f"half_in{g}_{'even' if h == 0 else 'odd'}") for h in range(2)] if LOAD * g < TWICE
                   else [sem(f"half_in{g}")] * 2 for g in range(LOADS)]

        def fills(g, b, h):
            return 32 * (b + 1) if LOAD * g < TWICE else 32 * (2 * b + h + 1)

        dense_in, out_written = sem("dense_in"), sem("out_written")
        ident_ready, fold_ready, w0_ready = sem("ident_ready"), sem("fold_ready"), sem("w0_ready")
        transposed, x0t_ready = [sem("transposed_a"), sem("transposed_b")], sem("x0t_ready")
        spread_ready = sem("spread_ready")
        z0_ready, zv_ready, zp_ready = sem("z0_ready"), sem("zv_ready"), sem("zp_ready")
        z0_used, zv_used, zp_used = sem("z0_used"), sem("zv_used"), sem("zp_used")
        xp_ready = [sem("x1_ps_ready"), sem("x2_ps_ready")]
        xs_ready = [sem("x1_sb_ready"), sem("x2_sb_ready")]
        evacuated = sem("evacuated")
        pooled_ready = sem("pooled_ready")
        fold_done, top_z_ready = sem("fold_done"), sem("top_z_ready")
        h1_done, h1_ready = sem("h1_done"), sem("h1_ready")
        h2_done, h2_ready = sem("h2_done"), sem("h2_ready")
        y_done, y_ready = sem("y_done"), sem("y_ready")

        LAST = BLOCKS - 1


        block = ctx.enter_context(nc.Block())

        @block.sync
        def _(sp):
            ids_b = ids.rearrange("(n p) f -> n p f", p=BLOCK)

            def load_idx(part, b):
                sp.dma_start(idx[part][:, :], ids_b[b, :, part * PART:(part + 1) * PART]).then_inc(idx_in[part], 16)

            def load_quad(b, h):
                sp.dma_start(x0_quad[:, :], x0_rows(b, 0, h * STEP, [[COLS, FIELDS], [0, 4], [1, STEP]])
                             ).then_inc(quad_in, 16)

            def load_rot(b, h, t):
                first, by = DELTAS[t]
                sp.dma_start(x0_rot[:, t, :],
                             x0_rows(b, first, h * STEP, [[COLS, FIELDS], [by * COLS, 4], [1, STEP]])
                             ).then_inc(rot_in[t], 16)

            def load_spread(b, h, g):
                tiles, at = spread(LOAD * g, h)
                for odd in (1, 0):
                    rows = HID // 2 if odd else HID
                    for field in range(2):
                        sp.dma_start(tiles[HID * field:HID * field + rows, at + odd:at + odd + LOAD - 1:2, :],
                                     x0_rows(b, 2 * (LOAD * g + odd) + field, h * STEP,
                                             [[0, rows], [4 * COLS, LOAD // 2], [1, STEP]])
                                     ).then_inc((half_in if odd else full_in)[g][h], 16)

            def write_scratch(b):
                for half in range(2):
                    sp.dma_start(x0_rows(b, half * FIELDS, 0, [[BLOCK, P], [FIELD_GROUP * COLS, FIELD_GROUPS], [1, BLOCK]]),
                                 x0t[:, :, :]).then_inc(scratch_written, 16)

            sp.dma_start(idx_first[:, :], ids_b[0, :, :]).then_inc(idx_first_in, 16)
            load_idx(0, 1)
            load_idx(1, 1)
            for dst, src in ((w0[:, :, :], w0a), (w0_mirror[:, :, :], w0b), (wk[0][:, :, :], w1),
                             (wk[1][:, :, :], w2), (wt1[:, 0, :], w_top1[0:P, :]),
                             (wt1[0:REST + DIM, 1, :], w_top1[P:Z_COLS + DIM, :]),
                             (wt2[:, :, :], w_top2.rearrange("(t p) n -> p t n", p=P)),
                             (wt3[:, 0, :], w_top3[0:P, :]), (wt3[:, 1, :], w_top3[P:2 * P, :]),
                             (bt1[:, :], b_top1), (bt2[:, :], b_top2)):
                sp.dma_start(dst, src).then_inc(w_in, 16)
            sp.wait_ge(x0t_ready, 1)
            write_scratch(0)
            sp.wait_ge(scratch_written, 16 * SCRATCH_DMAS)
            load_quad(0, 0)
            for t in range(T0):
                load_rot(0, 0, t)
            for g in range(LOADS):
                load_spread(0, 0, g)
            sp.wait_ge(gathered[0], 16 * PART)
            load_idx(0, 2)
            sp.wait_ge(z0_ready, T0)
            load_quad(0, 1)
            for t in range(T0):
                load_rot(0, 1, t)

            def half(i, h):
                s = 2 * i + h
                next_b, next_h = (i, 1) if h == 0 else (i + 1, 0)
                more = not (isinstance(i, int) and i >= LAST)
                if h == 1 and not more:
                    return
                for g in range(TWICE // LOAD):
                    if not (isinstance(s, int) and s == 0):
                        sp.wait_ge(zp_used, NP * (2 * s - 1) + (g + 1))
                    load_spread(next_b, next_h, g)
                if h == 0:
                    if not (isinstance(i, int) and i >= LAST - 1):
                        sp.wait_ge(gathered[1], 16 * PART * (i + 1))
                        load_idx(1, i + 2)
                    if more:
                        sp.wait_ge(x0t_ready, i + 2)
                        write_scratch(i + 1)
                        sp.wait_ge(scratch_written, 16 * SCRATCH_DMAS * (i + 2))
                if more:
                    sp.wait_ge(z0_ready, T0 * (s + 2))
                    load_quad(i + 1, h)
                    for t in range(2):
                        load_rot(i + 1, h, t)
                for g in range(TWICE // LOAD, LOADS):
                    sp.wait_ge(zp_used, NP * (2 * s + 1) + (g + 1))
                    load_spread(next_b, next_h, g)
                if more:
                    for t in range(2, T0):
                        load_rot(i + 1, h, t)
                if h == 1:
                    if not (isinstance(i, int) and i == 0):
                        sp.wait_ge(h1_done, i)
                    sp.dma_start(top_z[REST:REST + DIM, 1, :], dense_t[:, bass.ds(i * BLOCK, BLOCK)]
                                 ).then_inc(dense_in, 16)
                if h == 1 and not (isinstance(i, int) and i >= LAST - 2):
                    sp.wait_ge(gathered[0], 16 * PART * (i + 2))
                    load_idx(0, i + 3)

            half(0, 0)
            half(0, 1)
            with sp.Fori(1, LAST - 2) as i:
                half(i, 0)
                half(i, 1)
            for i in range(LAST - 2, LAST + 1):
                half(i, 0)
                half(i, 1)
            sp.wait_ge(h1_done, LAST)
            sp.dma_start(top_z[REST:REST + DIM, 1, :], dense_t[:, LAST * BLOCK:BATCH]).then_inc(dense_in, 16)
            sp.wait_ge(out_written, 16 * BLOCKS)

        @block.gpsimd
        def _(pool):
            def gather(f, idx_ap, done):
                nc.gpsimd.indirect_dma_start(emb[:, f, :], None, tables[f],
                                             bass.IndirectOffsetOnAxis(ap=idx_ap, axis=0)).then_inc(done, 16)

            def gather_part(part, n):
                gather(part * PART + n, idx[part][:, n:n + 1], gathered[part])

            def product(layer, j, k, parity):
                tiles, at = spread(j, parity)
                nc.gpsimd.tensor_tensor(out=zp[:, k, :], in0=tiles[:, at, :], in1=xs[layer - 1][:, :],
                                        op=ALU.mult).then_inc(zp_ready, 1)

            nc.gpsimd.memset(ident[:, :], 0.0).then_inc(ident_ready, 1)
            nc.gpsimd.memset(fold[:, :], 0.0).then_inc(fold_ready, 1)
            pool.wait_ge(ident_ready, 1)
            nc.gpsimd.affine_select(out=ident[:, :], in_=ident[:, :], compare_op=ALU.not_equal, fill=1.0, base=0,
                                    pattern=[[-1, P]], channel_multiplier=1).then_inc(ident_ready, 1)
            pool.wait_ge(idx_first_in, 16)
            for f in range(FIELDS):
                gather(f, idx_first[:, f:f + 1], first_gathered)
            for n, base in enumerate((0, -HID)):
                pool.wait_ge(fold_ready, n + 1)
                nc.gpsimd.affine_select(out=fold[:, :], in_=fold[:, :], compare_op=ALU.not_equal, fill=1.0, base=base,
                                        pattern=[[-1, HID]], channel_multiplier=1).then_inc(fold_ready, 1)
            for part in range(2):
                pool.wait_ge(idx_in[part], 16)
                pool.wait_ge(transposed[part], 1)
                for n in range(PART):
                    gather_part(part, n)
            pool.wait_ge(transposed[0], 2)
            pool.wait_ge(idx_in[0], 32)

            def half(i, h):
                s = 2 * i + h
                last = isinstance(i, int) and i == LAST
                more = not (isinstance(i, int) and i >= LAST - 1)
                if more:
                    for n in range(PART - 2 * NP):
                        gather_part(h, n)
                for k, j in enumerate(POOL_TILES):
                    if more:
                        gather_part(h, PART - 2 * NP + k)
                    if k == 0:
                        pool.wait_ge(xs_ready[1], s + 1)
                    pool.wait_ge(zp_used, NP * (2 * s) + k + 1)
                    product(2, j, k, h)
                if last and h == 1:
                    return
                for k, j in enumerate(POOL_TILES):
                    if k == 0:
                        pool.wait_ge(xs_ready[0], s + 2)
                    if k == NP - 1 and more and (h == 0 or not (isinstance(i, int) and i == LAST - 2)):
                        pool.wait_ge(transposed[1 - h], i + (2 if h == 0 else 3))
                        pool.wait_ge(idx_in[1 - h], 16 * (i + (2 if h == 0 else 3)))
                    pool.wait_ge(zp_used, NP * (2 * s + 1) + k + 1)
                    pool.wait_ge(spread_ready, T1 // 2 * (s + 1) + odd_tiles(j))
                    product(1, j, k, 1 - h)
                    if more:
                        gather_part(h, PART - NP + k)

            half(0, 0)
            half(0, 1)
            with pool.Fori(1, LAST - 2) as i:
                half(i, 0)
                half(i, 1)
            for i in range(LAST - 2, LAST + 1):
                half(i, 0)
                half(i, 1)

        @block.vector
        def _(dve):
            dve.wait_ge(w_in, 16 * 11)
            nc.vector.tensor_tensor(out=w0[:, 0:SYMMETRIC, :], in0=w0[:, 0:SYMMETRIC, :], in1=w0_mirror[:, :, :],
                                    op=ALU.add).then_inc(w0_ready, 1)

            def layer0(step, parity):
                dve.wait_ge(quad_in, 16 * (step + 1))
                for t in range(T0):
                    dve.wait_ge(rot_in[t], 16 * (step + 1))
                    if not (isinstance(step, int) and step * T0 + t < RING_0):
                        dve.wait_ge(z0_used, step * T0 + (t + 1 - RING_0))
                    nc.vector.tensor_tensor(out=z0[:, (parity * T0 + t) % RING_0, :], in0=x0_quad[:, :],
                                            in1=x0_rot[:, t, :], op=ALU.mult).then_inc(z0_ready, 1)

            def layer(number, b, parity, run, all_tiles=False):
                step = 2 * b + parity
                dve.wait_ge(xp_ready[number - 1], step + 1)
                k = 0
                for j in range(T1) if all_tiles else DVE_TILES:
                    if number == 1 and j % 2:
                        dve.wait_ge(spread_ready, step * (T1 // 2) + odd_tiles(j))
                    elif number == 1:
                        dve.wait_ge(full_in[j // LOAD][parity], fills(j // LOAD, b, parity))
                    tiles, at = spread(j, parity)
                    if j in POOL_TILES:
                        slot, ready = zp[:, POOL_TILES.index(j), :], zp_ready
                    else:
                        if not (isinstance(run, int) and run * NV + k < RING_V):
                            dve.wait_ge(zv_used, run * NV + (k + 1 - RING_V))
                        slot, ready = zv[:, k % RING_V, :], zv_ready
                        k += 1
                    nc.vector.tensor_tensor(out=slot, in0=xp[number - 1][:, :], in1=tiles[:, at, :],
                                            op=ALU.mult).then_inc(ready, 1)

            def pool_dims(n, i, runs=None):
                dve.wait_ge(evacuated, runs or 6 * i + (3, 5, 7)[n])
                if n == 0 and not (isinstance(i, int) and i == 0):
                    dve.wait_ge(fold_done, i)
                nc.vector.tensor_reduce(out=pooled[:, n, :], in_=act_out[n][:, :, :].rearrange("p d b -> p b d"),
                                        axis=AX.X, op=ALU.add).then_inc(pooled_ready, 1)

            layer0(0, 0)
            layer(1, 0, 0, 0, all_tiles=True)

            def body(i):
                last = isinstance(i, int) and i == LAST
                layer0(2 * i + 1, 1)
                layer(2, i, 0, 4 * i + 1)
                layer(1, i, 1, 4 * i + 2)
                pool_dims(0, i)
                if not last:
                    layer0(2 * i + 2, 0)
                layer(2, i, 1, 4 * i + 3)
                pool_dims(1, i)
                if not last:
                    layer(1, i + 1, 0, 4 * i + 4)
                pool_dims(2, i, 6 * BLOCKS if last else None)

            body(0)
            with dve.Fori(1, LAST) as i:
                body(i)
            body(LAST)

        @block.scalar
        def _(act):
            def copy_x0t(b):
                act.wait_ge(transposed[1], b + 1)
                if not (isinstance(b, int) and b == 0):
                    act.wait_ge(scratch_written, 16 * SCRATCH_DMAS * b)
                nc.scalar.activation(x0t[:, :, :], pt[:, :, :], ACT.Copy).then_inc(x0t_ready, 1)

            def spread_halves(b, parity, g):
                act.wait_ge(half_in[g][parity], fills(g, b, parity))
                for j in range(LOAD * g + 1, LOAD * g + LOAD, 2):
                    tiles, at = spread(j, parity)
                    for q in (0, HID):
                        ins = nc.scalar.activation(tiles[q + 32:q + 64, at, :], tiles[q:q + 32, at, :], ACT.Copy)
                    ins.then_inc(spread_ready, 1)

            def evacuate(n, bank, consumed, count, h):
                act.wait_ge(consumed, count)
                if n < 2:
                    for operand, ready in ((xp[n], xp_ready[n]), (xs[n], xs_ready[n])):
                        for ab in range(2):
                            for dst in (0, HID):
                                ins = nc.scalar.activation(operand[dst:dst + HID, ab * BANK:(ab + 1) * BANK],
                                                           acc[bank][HID * ab:HID * ab + HID, :], ACT.Relu)
                        ins.then_inc(ready, 1)
                nc.scalar.activation(act_out[n][:, h * GROUP_D:(h + 1) * GROUP_D, :],
                                     acc[bank][:, :].rearrange("p (d b) -> p d b", d=GROUP_D),
                                     ACT.Relu).then_inc(evacuated, 1)

            def top_z_out(b):
                act.wait_ge(fold_done, b + 1)
                nc.scalar.activation(top_z[:, 0, :], top_ps[:, 0, :], ACT.Copy)
                nc.scalar.activation(top_z[0:REST, 1, :], top_ps[0:REST, 1, :], ACT.Copy).then_inc(top_z_ready, 1)

            def top_h1_out(b):
                act.wait_ge(h1_done, b + 1)
                for t in range(TOP1 // P):
                    ins = nc.scalar.activation(top_h1[:, t, :], top_ps[:, t, :], ACT.Relu, bias=bt1[:, t:t + 1])
                ins.then_inc(h1_ready, 1)

            def top_h2_out(b):
                act.wait_ge(h2_done, b + 1)
                for t in range(TOP2 // P):
                    ins = nc.scalar.activation(top_h2[:, t, :], top_ps[:, t, :], ACT.Relu, bias=bt2[:, t:t + 1])
                ins.then_inc(h2_ready, 1)

            def top_y_out(b):
                act.wait_ge(y_done, b + 1)
                if not (isinstance(b, int) and b == 0):
                    act.wait_ge(out_written, 16 * b)
                nc.scalar.activation(top_y[0:1, :], top_ps[0:1, 0, :], ACT.Copy).then_inc(y_ready, 1)
                act.wait_ge(y_ready, b + 1)
                act.dma_start(out[:, bass.ds(b * BLOCK, BLOCK)], top_y[0:1, :]).then_inc(out_written, 16)

            copy_x0t(0)
            spread_halves(0, 0, 0)
            evacuate(0, 0, z0_used, T0, 0)
            for g in range(1, LOADS):
                spread_halves(0, 0, g)

            def half(i, h):
                s = 2 * i + h
                first, last = isinstance(i, int) and i == 0, isinstance(i, int) and i == LAST
                end = last and h == 1
                evacuate(1, (1 + 3 * h) % 2, zp_used, NP * (2 * s + 1), h)
                if not end:
                    evacuate(0, (2 + 3 * h) % 2, z0_used, T0 * (s + 2), 1 - h)
                    if h == 0 and not last:
                        copy_x0t(i + 1)
                    for g in range(TWICE // LOAD):
                        spread_halves(i + h, 1 - h, g)
                if not first:
                    (top_z_out if h == 0 else top_h2_out)(i - 1)
                evacuate(2, (3 + 3 * h) % 2, zp_used, NP * (2 * s + 2), h)
                if not end:
                    for g in range(TWICE // LOAD, LOADS):
                        spread_halves(i + h, 1 - h, g)
                if not first:
                    (top_h1_out if h == 0 else top_y_out)(i - 1)

            half(0, 0)
            half(0, 1)
            half(1, 0)
            half(1, 1)
            with act.Fori(2, LAST) as i:
                half(i, 0)
                half(i, 1)
            half(LAST, 0)
            half(LAST, 1)
            for stage in (top_z_out, top_h1_out, top_h2_out, top_y_out):
                stage(LAST)

        @block.tensor
        def _(pe):
            by_group = emb[:, :, :].rearrange("p (g m) d -> p g (m d)", g=FIELD_GROUPS)

            def transpose_part(part, b):
                if not (isinstance(b, int) and b == 0):
                    pe.wait_ge(gathered[part], 16 * PART * b)
                    if part == 0:
                        pe.wait_ge(x0t_ready, b)
                for g in range(part * FIELD_GROUPS // 2, (part + 1) * FIELD_GROUPS // 2):
                    ins = nc.tensor.transpose(pt[:, g, :], by_group[:, g, :], ident[:, :])
                ins.then_inc(transposed[part], 1)

            def contract(bank, weights, z, first, last, used):
                for ab in range(2):
                    ins = nc.tensor.matmul(acc[bank][64 * ab:64 * ab + 64, :], weights,
                                           z[:, ab * BANK:(ab + 1) * BANK], start=first, stop=last)
                ins.then_inc(used, 1)

            def layer0(step, parity, bank):
                for t in range(T0):
                    pe.wait_ge(z0_ready, step * T0 + (t + 1))
                    contract(bank, w0[:, t, :], z0[:, (parity * T0 + t) % RING_0, :], t == 0, t == T0 - 1, z0_used)

            def layer(number, run, bank, between=()):
                k_v = k_p = 0
                between = dict(between)
                for j in range(T1):
                    if j in POOL_TILES:
                        pe.wait_ge(zp_ready, run * NP + (k_p + 1))
                        contract(bank, wk[number - 1][:, j, :], zp[:, k_p, :], j == 0, j == T1 - 1, zp_used)
                        k_p += 1
                    else:
                        pe.wait_ge(zv_ready, run * NV + (k_v + 1))
                        contract(bank, wk[number - 1][:, j, :], zv[:, k_v % RING_V, :], j == 0, j == T1 - 1, zv_used)
                        k_v += 1
                    if j in between:
                        work, b = between[j]
                        work(b)

            def top_fold(b):
                pe.wait_ge(pooled_ready, 3 * (b + 1))
                if isinstance(b, int) and b == LAST:
                    pe.wait_ge(y_ready, b)
                nc.tensor.matmul(top_ps[0:HID, 0, :], fold[:, :], pooled[:, 0, :], start=True, stop=True)
                nc.tensor.matmul(top_ps[HID:P, 0, :], fold[:, :], pooled[:, 1, :], start=True, stop=True)
                nc.tensor.matmul(top_ps[0:HID, 1, :], fold[:, :], pooled[:, 2, :], start=True, stop=True
                                 ).then_inc(fold_done, 1)

            def top_h1_mm(b):
                pe.wait_ge(dense_in, 16 * (b + 1))
                pe.wait_ge(top_z_ready, b + 1)
                for t in range(TOP1 // P):
                    nc.tensor.matmul(top_ps[:, t, :], wt1[:, 0, t * P:(t + 1) * P], top_z[:, 0, :],
                                     start=True, stop=False)
                    ins = nc.tensor.matmul(top_ps[:, t, :], wt1[0:REST + DIM, 1, t * P:(t + 1) * P],
                                           top_z[0:REST + DIM, 1, :], start=False, stop=True)
                ins.then_inc(h1_done, 1)

            def top_h2_mm(b):
                pe.wait_ge(h1_ready, b + 1)
                for u in range(TOP2 // P):
                    for t in range(TOP1 // P):
                        ins = nc.tensor.matmul(top_ps[:, u, :], wt2[:, t, u * P:(u + 1) * P], top_h1[:, t, :],
                                               start=(t == 0), stop=(t == TOP1 // P - 1))
                ins.then_inc(h2_done, 1)

            def top_y_mm(b):
                pe.wait_ge(h2_ready, b + 1)
                for u in range(TOP2 // P):
                    ins = nc.tensor.matmul(top_ps[0:1, 0, :], wt3[:, u, :], top_h2[:, u, :],
                                           start=(u == 0), stop=(u == TOP2 // P - 1))
                ins.then_inc(y_done, 1)

            pe.wait_ge(ident_ready, 2)
            pe.wait_ge(first_gathered, 16 * FIELDS)
            transpose_part(0, 0)
            transpose_part(1, 0)
            pe.wait_ge(w0_ready, 1)
            layer0(0, 0, 0)
            layer(1, 0, 1)
            transpose_part(0, 1)

            def half(i, h):
                s = 2 * i + h
                first, last = isinstance(i, int) and i == 0, isinstance(i, int) and i == LAST
                end = last and h == 1
                if not end:
                    pe.wait_ge(evacuated, 3 * s + 1)
                    layer0(s + 1, 1 - h, (2 + 3 * h) % 2)
                if h == 0 and not last:
                    transpose_part(1, i + 1)
                pe.wait_ge(evacuated, 3 * s + 2)
                top = [] if first else [(3, ((top_fold, top_h2_mm)[h], i - 1))]
                layer(2, 2 * s + 1, (3 + 3 * h) % 2, top)
                if not end:
                    pe.wait_ge(evacuated, 3 * s + 3)
                    top = [] if first else [(3, ((top_h1_mm, top_y_mm)[h], i - 1))]
                    if h == 1 and not (isinstance(i, int) and i >= LAST - 1):
                        top.append((7, (lambda b: transpose_part(0, b), i + 2)))
                    layer(1, 2 * s + 2, (4 + 3 * h) % 2, top)

            half(0, 0)
            half(0, 1)
            with pe.Fori(1, LAST - 1) as i:
                half(i, 0)
                half(i, 1)
            for i in (LAST - 1, LAST):
                half(i, 0)
                half(i, 1)
            top_y_mm(LAST - 1)
            for stage in (top_fold, top_h1_mm, top_h2_mm, top_y_mm):
                stage(LAST)


def kernel(**inputs):
    import numpy as np
    import concourse.bacc as bacc
    from concourse.bass_utils import run_bass_kernel_spmd

    def plain(name):
        return np.ascontiguousarray(inputs[name])

    W0 = plain("L0_rec_W0")
    m = np.arange(FIELDS)[:, None, None]
    delta = np.array([[first + by * i for first, by in DELTAS] for i in range(4)])[None, :, :]
    other = (m + delta) % FIELDS
    arrays = {"dense_t": np.ascontiguousarray(plain("dense_ctx").T), "ids": plain("ids")}
    for f in range(FIELDS):
        arrays[f"tbl_{f}"] = plain(f"tbl_{f}")
    arrays["w0a"] = np.ascontiguousarray(W0[m, other].reshape(P, T0, HID))
    arrays["w0b"] = np.ascontiguousarray(W0[other, m][:, :, :SYMMETRIC].reshape(P, SYMMETRIC, HID))
    for n in (1, 2):
        w = plain(f"L0_rec_W{n}").reshape(T1, P, HID)
        arrays[f"w{n}"] = np.ascontiguousarray(w.transpose(1, 0, 2))
    arrays["w_top1"] = plain("W_top1")
    arrays["b_top1"] = np.ascontiguousarray(plain("b_top1").reshape(TOP1 // P, P).T)
    arrays["w_top2"] = plain("W_top2")
    arrays["b_top2"] = np.ascontiguousarray(plain("b_top2").reshape(TOP2 // P, P).T)
    arrays["w_top3"] = plain("W_top3")

    nc = bacc.Bacc("TRN2", target_bir_lowering=False, num_devices=1)
    aps = {name: nc.dram_tensor(name, a.shape, mybir.dt.from_np(a.dtype), kind="ExternalInput").ap()
           for name, a in arrays.items()}
    out = nc.dram_tensor("out", (1, BATCH), mybir.dt.float32, kind="ExternalOutput").ap()
    build(nc, aps["dense_t"], aps["ids"], [aps[f"tbl_{f}"] for f in range(FIELDS)], aps["w0a"], aps["w0b"],
          aps["w1"], aps["w2"], aps["w_top1"], aps["b_top1"], aps["w_top2"], aps["b_top2"], aps["w_top3"], out)
    r = run_bass_kernel_spmd(nc, [arrays], core_ids=[0])
    return r.results[0]["out"].reshape(BATCH, 1)
```

```python
import concourse.bass as bass
from concourse import mybir
from contextlib import ExitStack

BATCH, FIELDS, DIM, HID = 2048, 32, 16, 64
P = 128
BLOCK = P
BLOCKS = BATCH // BLOCK
BANK = 512
GROUP_D = BANK // BLOCK
GROUPS = DIM // GROUP_D
STEP = 2 * BANK
STEPS_PER_BLOCK = GROUPS // 2
COLS = DIM * BLOCK
FIELD_GROUP = P // DIM
FIELD_GROUPS = FIELDS // FIELD_GROUP
SCRATCH_DMAS = 2
DUP = 2 * FIELDS

DELTAS = [(1, 2), (2, 4), (9, 2), (0, 4), (16, 4)]
SYMMETRIC = 3
T0 = len(DELTAS)
T1 = FIELDS // 2
LOAD = 4
LOADS = T1 // LOAD

POOL_EVERY = 4
POOL_TILES = [j for j in range(T1) if j % POOL_EVERY == POOL_EVERY - 1]
DVE_TILES = [j for j in range(T1) if j % POOL_EVERY != POOL_EVERY - 1]
NV, NP = len(DVE_TILES), len(POOL_TILES)
ORDER = [list(range(T1)), list(range(T1 // 2, T1)) + list(range(T1 // 2))]
assert LOAD == POOL_EVERY
RING = 5
FIRST_TILES, STEP_TILES = T0 + NV, T0 + 2 * NV
TWICE = T1 // 2

assert FIELD_GROUPS == LOADS
PART = FIELDS // 2
GATHERS = ([4, 1, 1, 1], [3, 3, 1, 2])
GATHERS_FIRST = ([4, 1, 1, 1], [2, 2, 2, 3])
FIRST_AHEAD = 5
assert sum(map(sum, GATHERS)) == sum(map(sum, GATHERS_FIRST)) == PART
TOP1, TOP2 = 512, 256
Z_COLS = 3 * HID
REST = Z_COLS - P


def slot_free(n, before):
    return n + 1 - RING if n >= RING else max(k for k in range(1 - RING, 1) if (k - 1 + before) % RING == n)


def odd_tiles(j):
    return (j + 1) // 2


def build(nc, dense_t, ids, tables, w0a, w0b, w1, w2, w_top1, b_top1, w_top2, b_top2, w_top3, out):
    F32, I32 = mybir.dt.float32, mybir.dt.int32
    ALU, ACT, AX = mybir.AluOpType, mybir.ActivationFunctionType, mybir.AxisListType

    scratch = nc.dram_tensor("x0_rows", (BLOCKS, DUP, COLS), F32, kind="Internal")

    def x0_rows(block, row, column, pattern):
        return bass.AP(scratch, block * (DUP * COLS) + (row * COLS + column), pattern)

    ctx = ExitStack()
    with ctx:
        def sb(name, shape, dt=F32):
            return ctx.enter_context(nc.sbuf_tensor(name, shape, dt))

        def pb(name, shape, dt=F32):
            return ctx.enter_context(nc.psum_tensor(name, shape, dt))

        def sem(name):
            return ctx.enter_context(nc.semaphore(name))

        ident = sb("ident", [P, P])
        fold = sb("fold", [P, HID])
        w0 = sb("w0", [P, T0, HID])
        w0_mirror = sb("w0_mirror", [P, SYMMETRIC, HID])
        wk = [sb("w1_sb", [P, T1, HID]), sb("w2_sb", [P, T1, HID])]
        wt1 = sb("wt1", [P, 2, TOP1])
        wt2 = sb("wt2", [P, TOP1 // P, TOP2])
        wt3 = sb("wt3", [P, TOP2 // P, 1])
        bt1 = sb("bt1", [P, TOP1 // P])
        bt2 = sb("bt2", [P, TOP2 // P])

        idx_first = sb("idx_first", [P, FIELDS], I32)
        idx = [sb("idx_a", [P, PART], I32), sb("idx_b", [P, PART], I32)]
        emb = sb("emb", [P, FIELDS, DIM])
        x0t = sb("x0t", [P, FIELD_GROUPS, BLOCK])

        x0_quad = sb("x0_quad", [P, STEP])
        x0_rot = sb("x0_rot", [P, T0, STEP])
        spread_twice = [sb("spread_even", [P, TWICE, STEP]), sb("spread_odd", [P, TWICE, STEP])]
        spread_once = sb("spread_once", [P, T1 - TWICE, STEP])

        def spread(j, parity):
            return (spread_twice[parity], j) if j < TWICE else (spread_once, j - TWICE)

        xs = [sb("x1_sb", [P, STEP]), sb("x2_sb", [P, STEP])]
        zv = sb("zv", [P, RING, STEP])
        zp = sb("zp", [P, NP, STEP])
        act_out = [sb(f"act_out{n}", [P, STEPS_PER_BLOCK * GROUP_D, BLOCK]) for n in range(3)]
        pooled = sb("pooled", [P, 3, BLOCK])
        top_z = sb("top_z", [P, 2, BLOCK])
        top_h1 = sb("top_h1", [P, TOP1 // P, BLOCK])
        top_h2 = sb("top_h2", [P, TOP2 // P, BLOCK])
        top_y = sb("top_y", [1, BLOCK])

        acc = [pb("acc0", [P, BANK]), pb("acc1", [P, BANK])]
        xp = [pb("x1_ps", [P, STEP]), pb("x2_ps", [P, STEP])]
        pt = pb("pt", [P, FIELD_GROUPS, BLOCK])
        top_ps = pb("top_ps", [P, TOP1 // P, BLOCK])

        w_in = sem("w_in")
        idx_first_in, idx_in = sem("idx_first_in"), [sem("idx_a_in"), sem("idx_b_in")]
        first_gathered = [sem(f"first_gathered{g}") for g in range(FIELD_GROUPS)]
        first_transposed, first_x0t_ready = sem("first_transposed"), sem("first_x0t_ready")
        first_written = sem("first_written")
        gathered = [sem("gathered_a"), sem("gathered_b")]
        scratch_written = sem("scratch_written")
        quad_in = sem("quad_in")
        rot_in = [sem(f"rot_in{t}") for t in range(T0)]
        full_in = [[sem(f"full_in{g}_{'even' if h == 0 else 'odd'}") for h in range(2)] if LOAD * g < TWICE
                   else [sem(f"full_in{g}")] * 2 for g in range(LOADS)]
        half_in = [[sem(f"half_in{g}_{'even' if h == 0 else 'odd'}") for h in range(2)] if LOAD * g < TWICE
                   else [sem(f"half_in{g}")] * 2 for g in range(LOADS)]

        def fills(g, b, h):
            return 32 * (b + 1) if LOAD * g < TWICE else 32 * (2 * b + h + 1)

        dense_in, out_written = sem("dense_in"), sem("out_written")
        ident_ready, fold_ready, w0_ready = sem("ident_ready"), sem("fold_ready"), sem("w0_ready")
        transposed, x0t_ready = [sem("transposed_a"), sem("transposed_b")], sem("x0t_ready")
        spread_ready = sem("spread_ready")
        zv_ready, zp_ready = sem("zv_ready"), sem("zp_ready")
        zv_used, zp_used = sem("zv_used"), sem("zp_used")
        xp_ready = [sem("x1_ps_ready"), sem("x2_ps_ready")]
        xs_ready = [sem("x1_sb_ready"), sem("x2_sb_ready")]
        evacuated = sem("evacuated")
        pooled_ready = sem("pooled_ready")
        fold_done, top_z_ready = sem("fold_done"), sem("top_z_ready")
        h1_done, h1_ready = sem("h1_done"), sem("h1_ready")
        h2_done, h2_ready = sem("h2_done"), sem("h2_ready")
        y_done, y_ready = sem("y_done"), sem("y_ready")

        LAST = BLOCKS - 1


        block = ctx.enter_context(nc.Block())

        @block.sync
        def _(sp):
            ids_b = ids.rearrange("(n p) f -> n p f", p=BLOCK)

            def load_idx(part, b):
                sp.dma_start(idx[part][:, :], ids_b[b, :, part * PART:(part + 1) * PART]).then_inc(idx_in[part], 16)

            def load_quad(b, h):
                sp.dma_start(x0_quad[:, :], x0_rows(b, 0, h * STEP, [[COLS, FIELDS], [0, 4], [1, STEP]])
                             ).then_inc(quad_in, 16)

            def load_rot(b, h, t):
                first, by = DELTAS[t]
                sp.dma_start(x0_rot[:, t, :],
                             x0_rows(b, first, h * STEP, [[COLS, FIELDS], [by * COLS, 4], [1, STEP]])
                             ).then_inc(rot_in[t], 16)

            def load_first_rows(m):
                for dst, first, by, done in ((x0_quad[4 * m:4 * m + P // 2, :], 0, 0, quad_in),
                                             (x0_rot[4 * m:4 * m + P // 2, 0, :], *DELTAS[0], rot_in[0])):
                    sp.dma_start(dst, x0_rows(0, m + first, 0, [[COLS, FIELDS // 2], [by * COLS, 4], [1, STEP]])
                                 ).then_inc(done, 16)

            def load_spread(b, h, g):
                tiles, at = spread(LOAD * g, h)
                for odd in (1, 0):
                    rows = HID // 2 if odd else HID
                    for field in range(2):
                        sp.dma_start(tiles[HID * field:HID * field + rows, at + odd:at + odd + LOAD - 1:2, :],
                                     x0_rows(b, 2 * (LOAD * g + odd) + field, h * STEP,
                                             [[0, rows], [4 * COLS, LOAD // 2], [1, STEP]])
                                     ).then_inc((half_in if odd else full_in)[g][h], 16)

            def write_scratch(b):
                for half in range(2):
                    sp.dma_start(x0_rows(b, half * FIELDS, 0, [[BLOCK, P], [FIELD_GROUP * COLS, FIELD_GROUPS], [1, BLOCK]]),
                                 x0t[:, :, :]).then_inc(scratch_written, 16)

            sp.dma_start(idx_first[:, :], ids_b[0, :, :]).then_inc(idx_first_in, 16)
            load_idx(0, 1)
            load_idx(1, 1)
            for dst, src in ((w0[:, :, :], w0a), (w0_mirror[:, :, :], w0b), (wk[0][:, :, :], w1),
                             (wk[1][:, :, :], w2), (wt1[:, 0, :], w_top1[0:P, :]),
                             (wt1[0:REST + DIM, 1, :], w_top1[P:Z_COLS + DIM, :]),
                             (wt2[:, :, :], w_top2.rearrange("(t p) n -> p t n", p=P)),
                             (wt3[:, 0, :], w_top3[0:P, :]), (wt3[:, 1, :], w_top3[P:2 * P, :]),
                             (bt1[:, :], b_top1), (bt2[:, :], b_top2)):
                sp.dma_start(dst, src).then_inc(w_in, 16)
            for g in range(FIELD_GROUPS):
                sp.wait_ge(first_x0t_ready, g + 1)
                for half in range(2):
                    sp.dma_start(x0_rows(0, half * FIELDS + g * FIELD_GROUP, 0, [[BLOCK, P], [1, BLOCK]]),
                                 x0t[:, g, :]).then_inc(first_written, 16)
                sp.wait_ge(first_written, 16 * SCRATCH_DMAS * (g + 1))
                if g == FIELD_GROUPS - 2:
                    load_first_rows(0)
                if g == FIELD_GROUPS - 1:
                    load_first_rows(FIELDS // 2)
                    for t in range(1, T0):
                        load_rot(0, 0, t)
                load_spread(0, 0, g)
            sp.wait_ge(gathered[0], 16 * PART)
            load_idx(0, 2)
            sp.wait_ge(zv_ready, T0)
            load_quad(0, 1)
            for t in range(T0):
                load_rot(0, 1, t)

            def half(i, h):
                s = 2 * i + h
                next_b, next_h = (i, 1) if h == 0 else (i + 1, 0)
                more = not (isinstance(i, int) and i >= LAST)
                if h == 1 and not more:
                    return
                for g in range(TWICE // LOAD):
                    if not (isinstance(s, int) and s == 0):
                        sp.wait_ge(zp_used, NP * (2 * s - 1) + (LOADS - TWICE // LOAD + g + 1))
                    load_spread(next_b, next_h, g)
                if h == 0:
                    if not (isinstance(i, int) and i >= LAST - 1):
                        sp.wait_ge(gathered[1], 16 * PART * (i + 1))
                        load_idx(1, i + 2)

                def load_layer0():
                    if more:
                        if h == 0:
                            sp.wait_ge(x0t_ready, i + 1)
                            write_scratch(i + 1)
                            sp.wait_ge(scratch_written, 16 * SCRATCH_DMAS * (i + 1))
                        sp.wait_ge(zv_ready, FIRST_TILES + STEP_TILES * s + T0)
                        load_quad(i + 1, h)
                        for t in range(2):
                            load_rot(i + 1, h, t)

                if h == 1:
                    load_layer0()
                for g in range(TWICE // LOAD, LOADS):
                    sp.wait_ge(zp_used, NP * (2 * s + 1) + (g - TWICE // LOAD + 1))
                    load_spread(next_b, next_h, g)
                if h == 0:
                    load_layer0()
                if more:
                    for t in range(2, T0):
                        load_rot(i + 1, h, t)
                if h == 1:
                    if not (isinstance(i, int) and i == 0):
                        sp.wait_ge(h1_done, i)
                    sp.dma_start(top_z[REST:REST + DIM, 1, :], dense_t[:, bass.ds(i * BLOCK, BLOCK)]
                                 ).then_inc(dense_in, 16)
                if h == 1 and not (isinstance(i, int) and i >= LAST - 2):
                    sp.wait_ge(gathered[0], 16 * PART * (i + 2))
                    load_idx(0, i + 3)

            half(0, 0)
            half(0, 1)
            with sp.Fori(1, LAST - 2) as i:
                half(i, 0)
                half(i, 1)
            for i in range(LAST - 2, LAST + 1):
                half(i, 0)
                half(i, 1)
            sp.wait_ge(h1_done, LAST)
            sp.dma_start(top_z[REST:REST + DIM, 1, :], dense_t[:, LAST * BLOCK:BATCH]).then_inc(dense_in, 16)
            sp.wait_ge(out_written, 16 * BLOCKS)

        @block.gpsimd
        def _(pool):
            def gather(f, idx_ap, done):
                nc.gpsimd.indirect_dma_start(emb[:, f, :], None, tables[f],
                                             bass.IndirectOffsetOnAxis(ap=idx_ap, axis=0)).then_inc(done, 16)

            def gather_part(part, n):
                gather(part * PART + n, idx[part][:, n:n + 1], gathered[part])

            def product(layer, j, k, parity):
                tiles, at = spread(j, parity)
                nc.gpsimd.tensor_tensor(out=zp[:, k, :], in0=tiles[:, at, :], in1=xs[layer - 1][:, :],
                                        op=ALU.mult).then_inc(zp_ready, 1)

            nc.gpsimd.memset(ident[:, :], 0.0).then_inc(ident_ready, 1)
            nc.gpsimd.memset(fold[:, :], 0.0).then_inc(fold_ready, 1)
            pool.wait_ge(ident_ready, 1)
            nc.gpsimd.affine_select(out=ident[:, :], in_=ident[:, :], compare_op=ALU.not_equal, fill=1.0, base=0,
                                    pattern=[[-1, P]], channel_multiplier=1).then_inc(ident_ready, 1)
            pool.wait_ge(idx_first_in, 16)
            for f in range(FIELDS):
                gather(f, idx_first[:, f:f + 1], first_gathered[f // FIELD_GROUP])
            for n, base in enumerate((0, -HID)):
                pool.wait_ge(fold_ready, n + 1)
                nc.gpsimd.affine_select(out=fold[:, :], in_=fold[:, :], compare_op=ALU.not_equal, fill=1.0, base=base,
                                        pattern=[[-1, HID]], channel_multiplier=1).then_inc(fold_ready, 1)
            for part in range(2):
                pool.wait_ge(idx_in[part], 16)
                pool.wait_ge(first_transposed, FIELD_GROUPS // 2 * (part + 1))
                for n in range(PART if part == 0 else FIRST_AHEAD):
                    gather_part(part, n)
            pool.wait_ge(xs_ready[0], 1)
            for k, j in enumerate(POOL_TILES):
                pool.wait_ge(spread_ready, odd_tiles(j))
                product(1, j, k, 0)
                gather_part(1, FIRST_AHEAD + k)
            for n in range(FIRST_AHEAD + NP, PART):
                gather_part(1, n)
            pool.wait_ge(transposed[0], 1)
            pool.wait_ge(idx_in[0], 32)

            def half(i, h):
                s = 2 * i + h
                last = isinstance(i, int) and i == LAST
                more = not (isinstance(i, int) and i >= LAST - 1)
                ahead, behind = GATHERS_FIRST if isinstance(i, int) and s <= 1 else GATHERS
                n = 0
                for k, j in enumerate(j for j in ORDER[1] if j in POOL_TILES):
                    for _ in range(ahead[k] if more else 0):
                        gather_part(h, n)
                        n += 1
                    if k == 0:
                        pool.wait_ge(xs_ready[1], s + 1)
                    pool.wait_ge(zp_used, NP * (2 * s) + k + 1)
                    product(2, j, k, h)
                if last and h == 1:
                    return
                for k, j in enumerate(POOL_TILES):
                    if k == 0:
                        pool.wait_ge(xs_ready[0], s + 2)
                    if k == NP - 1 and more and (h == 0 or not (isinstance(i, int) and i == LAST - 2)):
                        pool.wait_ge(transposed[1 - h], i + (1 if h == 0 else 2))
                        pool.wait_ge(idx_in[1 - h], 16 * (i + (2 if h == 0 else 3)))
                    pool.wait_ge(zp_used, NP * (2 * s + 1) + k + 1)
                    pool.wait_ge(spread_ready, T1 // 2 * (s + 1) + odd_tiles(j))
                    product(1, j, k, 1 - h)
                    for _ in range(behind[k] if more else 0):
                        gather_part(h, n)
                        n += 1

            half(0, 0)
            half(0, 1)
            with pool.Fori(1, LAST - 2) as i:
                half(i, 0)
                half(i, 1)
            for i in range(LAST - 2, LAST + 1):
                half(i, 0)
                half(i, 1)

        @block.vector
        def _(dve):
            dve.wait_ge(w_in, 16 * 11)
            nc.vector.tensor_tensor(out=w0[:, 0:SYMMETRIC, :], in0=w0[:, 0:SYMMETRIC, :], in1=w0_mirror[:, :, :],
                                    op=ALU.add).then_inc(w0_ready, 1)

            def ring_tile(base, n, in0, in1):
                if isinstance(base, int) and base <= FIRST_TILES:
                    before = base
                else:
                    before = STEP_TILES
                if n >= RING or not (isinstance(base, int) and base == 0):
                    dve.wait_ge(zv_used, base + slot_free(n, before))
                nc.vector.tensor_tensor(out=zv[:, n % RING, :], in0=in0, in1=in1, op=ALU.mult
                                        ).then_inc(zv_ready, 1)

            def layer0(step, base):
                dve.wait_ge(quad_in, 16 * (step + 2))
                for t in range(T0):
                    dve.wait_ge(rot_in[t], 16 * (step + (2 if t == 0 else 1)))
                    ring_tile(base, t, x0_quad[:, :], x0_rot[:, t, :])

            def layer(number, b, parity, base, n):
                step = 2 * b + parity
                dve.wait_ge(xp_ready[number - 1], step + 1)
                for j in [j for j in ORDER[number - 1] if j in DVE_TILES]:
                    if number == 1 and j % 2:
                        dve.wait_ge(spread_ready, step * (T1 // 2) + odd_tiles(j))
                    elif number == 1:
                        dve.wait_ge(full_in[j // LOAD][parity], fills(j // LOAD, b, parity))
                    tiles, at = spread(j, parity)
                    ring_tile(base, n, xp[number - 1][:, :], tiles[:, at, :])
                    n += 1

            def pool_dims(n, i, runs=None):
                dve.wait_ge(evacuated, runs or 6 * i + (3, 5, 7)[n])
                if n == 0 and not (isinstance(i, int) and i == 0):
                    dve.wait_ge(fold_done, i)
                nc.vector.tensor_reduce(out=pooled[:, n, :], in_=act_out[n][:, :, :].rearrange("p d b -> p b d"),
                                        axis=AX.X, op=ALU.add).then_inc(pooled_ready, 1)

            layer0(0, 0)
            layer(1, 0, 0, 0, T0)

            def body(i):
                last = isinstance(i, int) and i == LAST
                for h in range(2):
                    base = FIRST_TILES + STEP_TILES * (2 * i + h)
                    end = last and h == 1
                    if not end:
                        layer0(2 * i + h + 1, base)
                    layer(2, i, h, base, 0 if end else T0)
                    if h == 1:
                        pool_dims(1, i)
                    if not end:
                        layer(1, i + h, 1 - h, base, T0 + NV)
                    if h == 0:
                        pool_dims(0, i)
                pool_dims(2, i, 6 * BLOCKS if last else None)

            body(0)
            with dve.Fori(1, LAST) as i:
                body(i)
            body(LAST)

        @block.scalar
        def _(act):
            def copy_x0t(b):
                act.wait_ge(transposed[1], b)
                if isinstance(b, int) and b == 1:
                    act.wait_ge(first_written, 16 * SCRATCH_DMAS * FIELD_GROUPS)
                else:
                    act.wait_ge(scratch_written, 16 * SCRATCH_DMAS * (b - 1))
                nc.scalar.activation(x0t[:, :, :], pt[:, :, :], ACT.Copy).then_inc(x0t_ready, 1)

            def spread_halves(b, parity, g):
                act.wait_ge(half_in[g][parity], fills(g, b, parity))
                for j in range(LOAD * g + 1, LOAD * g + LOAD, 2):
                    tiles, at = spread(j, parity)
                    for q in (0, HID):
                        ins = nc.scalar.activation(tiles[q + 32:q + 64, at, :], tiles[q:q + 32, at, :], ACT.Copy)
                    ins.then_inc(spread_ready, 1)

            def evacuate(n, bank, consumed, count, h):
                act.wait_ge(consumed, count)
                if n < 2:
                    for operand, ready in ((xp[n], xp_ready[n]), (xs[n], xs_ready[n])):
                        for ab in range(2):
                            for dst in (0, HID):
                                ins = nc.scalar.activation(operand[dst:dst + HID, ab * BANK:(ab + 1) * BANK],
                                                           acc[bank][HID * ab:HID * ab + HID, :], ACT.Relu)
                        ins.then_inc(ready, 1)
                nc.scalar.activation(act_out[n][:, h * GROUP_D:(h + 1) * GROUP_D, :],
                                     acc[bank][:, :].rearrange("p (d b) -> p d b", d=GROUP_D),
                                     ACT.Relu).then_inc(evacuated, 1)

            def top_z_out(b):
                act.wait_ge(fold_done, b + 1)
                nc.scalar.activation(top_z[:, 0, :], top_ps[:, 0, :], ACT.Copy)
                nc.scalar.activation(top_z[0:REST, 1, :], top_ps[0:REST, 1, :], ACT.Copy).then_inc(top_z_ready, 1)

            def top_h1_out(b):
                act.wait_ge(h1_done, b + 1)
                for t in range(TOP1 // P):
                    ins = nc.scalar.activation(top_h1[:, t, :], top_ps[:, t, :], ACT.Relu, bias=bt1[:, t:t + 1])
                ins.then_inc(h1_ready, 1)

            def top_h2_out(b):
                act.wait_ge(h2_done, b + 1)
                for t in range(TOP2 // P):
                    ins = nc.scalar.activation(top_h2[:, t, :], top_ps[:, t, :], ACT.Relu, bias=bt2[:, t:t + 1])
                ins.then_inc(h2_ready, 1)

            def top_y_out(b):
                act.wait_ge(y_done, b + 1)
                if not (isinstance(b, int) and b == 0):
                    act.wait_ge(out_written, 16 * b)
                nc.scalar.activation(top_y[0:1, :], top_ps[0:1, 0, :], ACT.Copy).then_inc(y_ready, 1)
                act.wait_ge(y_ready, b + 1)
                act.dma_start(out[:, bass.ds(b * BLOCK, BLOCK)], top_y[0:1, :]).then_inc(out_written, 16)

            for g in range(FIELD_GROUPS):
                act.wait_ge(first_transposed, g + 1)
                nc.scalar.activation(x0t[:, g, :], pt[:, g, :], ACT.Copy).then_inc(first_x0t_ready, 1)
                if g > 0:
                    spread_halves(0, 0, g - 1)
            evacuate(0, 0, zv_used, T0, 0)
            spread_halves(0, 0, LOADS - 1)

            def half(i, h):
                s = 2 * i + h
                first, last = isinstance(i, int) and i == 0, isinstance(i, int) and i == LAST
                end = last and h == 1
                evacuate(1, (1 + 3 * h) % 2, zp_used, NP * (2 * s + 1), h)
                if not end:
                    evacuate(0, (2 + 3 * h) % 2, zv_used, FIRST_TILES + STEP_TILES * s + T0, 1 - h)
                    if h == 0 and not last:
                        copy_x0t(i + 1)
                    for g in range(TWICE // LOAD):
                        spread_halves(i + h, 1 - h, g)
                if not first:
                    (top_z_out if h == 0 else top_h2_out)(i - 1)
                if not end:
                    for g in range(TWICE // LOAD, LOADS):
                        spread_halves(i + h, 1 - h, g)
                evacuate(2, (3 + 3 * h) % 2, zp_used, NP * (2 * s + 2), h)
                if not first:
                    (top_h1_out if h == 0 else top_y_out)(i - 1)

            half(0, 0)
            half(0, 1)
            half(1, 0)
            half(1, 1)
            with act.Fori(2, LAST) as i:
                half(i, 0)
                half(i, 1)
            half(LAST, 0)
            half(LAST, 1)
            for stage in (top_z_out, top_h1_out, top_h2_out, top_y_out):
                stage(LAST)

        @block.tensor
        def _(pe):
            by_group = emb[:, :, :].rearrange("p (g m) d -> p g (m d)", g=FIELD_GROUPS)

            def transpose_part(part, b):
                pe.wait_ge(gathered[part], 16 * PART * b)
                if part == 0 and isinstance(b, int) and b == 1:
                    pe.wait_ge(first_x0t_ready, FIELD_GROUPS)
                elif part == 0:
                    pe.wait_ge(x0t_ready, b - 1)
                for g in range(part * FIELD_GROUPS // 2, (part + 1) * FIELD_GROUPS // 2):
                    ins = nc.tensor.transpose(pt[:, g, :], by_group[:, g, :], ident[:, :])
                ins.then_inc(transposed[part], 1)

            def contract(bank, weights, z, first, last, used):
                for ab in range(2):
                    ins = nc.tensor.matmul(acc[bank][64 * ab:64 * ab + 64, :], weights,
                                           z[:, ab * BANK:(ab + 1) * BANK], start=first, stop=last)
                ins.then_inc(used, 1)

            def layer0(base, bank):
                for t in range(T0):
                    pe.wait_ge(zv_ready, base + (t + 1))
                    contract(bank, w0[:, t, :], zv[:, t % RING, :], t == 0, t == T0 - 1, zv_used)

            def layer(number, run, base, k, bank, between=()):
                k_p = 0
                between = dict(between)
                for n, j in enumerate(ORDER[number - 1]):
                    if j in POOL_TILES:
                        pe.wait_ge(zp_ready, run * NP + (k_p + 1))
                        contract(bank, wk[number - 1][:, j, :], zp[:, k_p, :], n == 0, n == T1 - 1, zp_used)
                        k_p += 1
                    else:
                        pe.wait_ge(zv_ready, base + (k + 1))
                        contract(bank, wk[number - 1][:, j, :], zv[:, k % RING, :], n == 0, n == T1 - 1, zv_used)
                        k += 1
                    if n in between:
                        work, b = between[n]
                        work(b)

            def top_fold(b):
                pe.wait_ge(pooled_ready, 3 * (b + 1))
                if isinstance(b, int) and b == LAST:
                    pe.wait_ge(y_ready, b)
                nc.tensor.matmul(top_ps[0:HID, 0, :], fold[:, :], pooled[:, 0, :], start=True, stop=True)
                nc.tensor.matmul(top_ps[HID:P, 0, :], fold[:, :], pooled[:, 1, :], start=True, stop=True)
                nc.tensor.matmul(top_ps[0:HID, 1, :], fold[:, :], pooled[:, 2, :], start=True, stop=True
                                 ).then_inc(fold_done, 1)

            def top_h1_mm(b):
                pe.wait_ge(dense_in, 16 * (b + 1))
                pe.wait_ge(top_z_ready, b + 1)
                for t in range(TOP1 // P):
                    nc.tensor.matmul(top_ps[:, t, :], wt1[:, 0, t * P:(t + 1) * P], top_z[:, 0, :],
                                     start=True, stop=False)
                    ins = nc.tensor.matmul(top_ps[:, t, :], wt1[0:REST + DIM, 1, t * P:(t + 1) * P],
                                           top_z[0:REST + DIM, 1, :], start=False, stop=True)
                ins.then_inc(h1_done, 1)

            def top_h2_mm(b):
                pe.wait_ge(h1_ready, b + 1)
                for u in range(TOP2 // P):
                    for t in range(TOP1 // P):
                        ins = nc.tensor.matmul(top_ps[:, u, :], wt2[:, t, u * P:(u + 1) * P], top_h1[:, t, :],
                                               start=(t == 0), stop=(t == TOP1 // P - 1))
                ins.then_inc(h2_done, 1)

            def top_y_mm(b):
                pe.wait_ge(h2_ready, b + 1)
                for u in range(TOP2 // P):
                    ins = nc.tensor.matmul(top_ps[0:1, 0, :], wt3[:, u, :], top_h2[:, u, :],
                                           start=(u == 0), stop=(u == TOP2 // P - 1))
                ins.then_inc(y_done, 1)

            pe.wait_ge(ident_ready, 2)
            for g in range(FIELD_GROUPS):
                pe.wait_ge(first_gathered[g], 16 * FIELD_GROUP)
                if g > 0:
                    pe.wait_ge(first_x0t_ready, g)
                nc.tensor.transpose(pt[:, g, :], by_group[:, g, :], ident[:, :]).then_inc(first_transposed, 1)
            pe.wait_ge(w0_ready, 1)
            layer0(0, 0)
            layer(1, 0, 0, T0, 1)
            transpose_part(0, 1)

            def half(i, h):
                s = 2 * i + h
                first, last = isinstance(i, int) and i == 0, isinstance(i, int) and i == LAST
                end = last and h == 1
                base = FIRST_TILES + STEP_TILES * s
                if not end:
                    pe.wait_ge(evacuated, 3 * s + 1)
                    layer0(base, (2 + 3 * h) % 2)
                if h == 0 and not last:
                    transpose_part(1, i + 1)
                if not end:
                    pe.wait_ge(evacuated, 3 * s + 2)
                top = [] if first else [(3, ((top_fold, top_h2_mm)[h], i - 1))]
                if end:
                    top_h2_mm(LAST - 1)
                    pe.wait_ge(evacuated, 3 * s + 2)
                    top = [(7, (top_y_mm, LAST - 1))]
                layer(2, 2 * s + 1, base, 0 if end else T0, (3 + 3 * h) % 2, top)
                if not end:
                    pe.wait_ge(evacuated, 3 * s + 3)
                    top = [] if first else [(3, ((top_h1_mm, top_y_mm)[h], i - 1))]
                    if h == 1 and not (isinstance(i, int) and i >= LAST - 1):
                        top.append((7, (lambda b: transpose_part(0, b), i + 2)))
                    layer(1, 2 * s + 2, base, T0 + NV, (4 + 3 * h) % 2, top)

            half(0, 0)
            half(0, 1)
            with pe.Fori(1, LAST - 1) as i:
                half(i, 0)
                half(i, 1)
            for i in (LAST - 1, LAST):
                half(i, 0)
                half(i, 1)
            for stage in (top_fold, top_h1_mm, top_h2_mm, top_y_mm):
                stage(LAST)


def kernel(**inputs):
    import numpy as np
    import concourse.bacc as bacc
    from concourse.bass_utils import run_bass_kernel_spmd

    def plain(name):
        return np.ascontiguousarray(inputs[name])

    W0 = plain("L0_rec_W0")
    m = np.arange(FIELDS)[:, None, None]
    delta = np.array([[first + by * i for first, by in DELTAS] for i in range(4)])[None, :, :]
    other = (m + delta) % FIELDS
    arrays = {"dense_t": np.ascontiguousarray(plain("dense_ctx").T), "ids": plain("ids")}
    for f in range(FIELDS):
        arrays[f"tbl_{f}"] = plain(f"tbl_{f}")
    arrays["w0a"] = np.ascontiguousarray(W0[m, other].reshape(P, T0, HID))
    arrays["w0b"] = np.ascontiguousarray(W0[other, m][:, :, :SYMMETRIC].reshape(P, SYMMETRIC, HID))
    for n in (1, 2):
        w = plain(f"L0_rec_W{n}").reshape(T1, P, HID)
        arrays[f"w{n}"] = np.ascontiguousarray(w.transpose(1, 0, 2))
    arrays["w_top1"] = plain("W_top1")
    arrays["b_top1"] = np.ascontiguousarray(plain("b_top1").reshape(TOP1 // P, P).T)
    arrays["w_top2"] = plain("W_top2")
    arrays["b_top2"] = np.ascontiguousarray(plain("b_top2").reshape(TOP2 // P, P).T)
    arrays["w_top3"] = plain("W_top3")

    nc = bacc.Bacc("TRN2", target_bir_lowering=False, num_devices=1)
    aps = {name: nc.dram_tensor(name, a.shape, mybir.dt.from_np(a.dtype), kind="ExternalInput").ap()
           for name, a in arrays.items()}
    out = nc.dram_tensor("out", (1, BATCH), mybir.dt.float32, kind="ExternalOutput").ap()
    build(nc, aps["dense_t"], aps["ids"], [aps[f"tbl_{f}"] for f in range(FIELDS)], aps["w0a"], aps["w0b"],
          aps["w1"], aps["w2"], aps["w_top1"], aps["b_top1"], aps["w_top2"], aps["b_top2"], aps["w_top3"], out)
    r = run_bass_kernel_spmd(nc, [arrays], core_ids=[0])
    return r.results[0]["out"].reshape(BATCH, 1)
```
